# Optimizing a Trainium2 kernel written in Bass

```python
import numpy as np
import jax
import jax.numpy as jnp

def _softmax(x, axis=-1):
    return jax.nn.softmax(x, axis=axis)

def _gelu(x):
    return jax.nn.gelu(x, approximate=True)

def _silu(x):
    return jax.nn.silu(x)

def _sigmoid(x):
    return jax.nn.sigmoid(x)

def _layernorm(x, axis=-1, eps=1e-05):
    m = jnp.mean(x, axis=axis, keepdims=True)
    v = jnp.var(x, axis=axis, keepdims=True)
    return (x - m) / jnp.sqrt(v + eps)

def _scatter_add(tgt, idx, src, axis=0):
    return tgt.at[idx].add(src)

def _segment_sum(src, seg, n):
    return jax.ops.segment_sum(src, seg, n)
kernel_name = 'mk_gnn_preln_d2_gnn_r32_5c0507'

def setup_inputs(seed: int=0):
    np.random.seed(seed)
    _w = jnp.asarray

    def _rec_inputs():
        import jax
        import jax.numpy as jnp
        _gk = jax.random.key(seed)
        x = -0.000202 + 1 * jax.random.normal(jax.random.fold_in(_gk, 1), (3125, 64), jnp.float32)
        _s = jax.random.randint(jax.random.fold_in(_gk, 2), (50000,), 0, 3125, jnp.int32)
        _d = jax.random.randint(jax.random.fold_in(_gk, 3), (50000,), 0, 3125, jnp.int32)
        _loop = jnp.arange(3125, dtype=jnp.int32)
        src = jnp.concatenate([_s, _d, _loop])
        dst = jnp.concatenate([_d, _s, _loop])
        _o = jnp.argsort(dst, stable=True)
        src = src[_o]
        dst = dst[_o]
        edge_weight1 = -0.000414295 + 0.999828 * jax.random.normal(jax.random.fold_in(_gk, 13), (103125, 1), jnp.float32)
        return (x, src, dst, edge_weight1)
    x, src, dst, edge_weight1 = _rec_inputs()

    def _L0_gnn_setup():
        import jax, jax.numpy as jnp
        import numpy as np
        N_NODES = 3125
        N_EDGES = 50000
        IN_FEAT = 64
        OUT_FEAT = 64
        key = jax.random.key(seed)
        k1, k2, k3, k4, k5 = jax.random.split(key, 5)
        x = jax.random.normal(k1, (N_NODES, IN_FEAT), dtype=jnp.float32)
        row = jax.random.randint(k2, (N_EDGES,), 0, N_NODES, dtype=jnp.int32)
        col = jax.random.randint(k3, (N_EDGES,), 0, N_NODES, dtype=jnp.int32)
        col = jnp.where(col == row, (col + 1) % N_NODES, col)
        edge_index = jnp.stack([row, col], axis=0)
        W = jax.random.normal(k4, (2, IN_FEAT, OUT_FEAT), dtype=jnp.float32) * 0.05
        b = jax.random.normal(k5, (OUT_FEAT,), dtype=jnp.float32) * 0.05
        return {'x': x, 'edge_index': edge_index, 'W': W, 'b': b}
    _L0_gnn_all = _L0_gnn_setup()
    _L0_gnn_in = {k: v for k, v in _L0_gnn_all.items() if k in ('W', 'b')}
    del _L0_gnn_all

    def _L1_gnn_setup():
        import jax, jax.numpy as jnp
        import numpy as np
        N = 3125
        E = 50000
        H = 64
        T = 2

        def gru_cell(x, h, W_ih_t, W_hh_t, b_ih_t, b_hh_t):
            gi = x @ W_ih_t.T + b_ih_t
            gh = h @ W_hh_t.T + b_hh_t
            ir, iz, inn = jnp.split(gi, 3, axis=1)
            hr, hz, hn = jnp.split(gh, 3, axis=1)
            r = jax.nn.sigmoid(ir + hr)
            z = jax.nn.sigmoid(iz + hz)
            n = jnp.tanh(inn + r * hn)
            return (1.0 - z) * n + z * h
        key = jax.random.key(seed)
        ks = jax.random.split(key, 12)
        hv = jax.random.normal(ks[0], (N, H), dtype=jnp.float32)
        he = jax.random.normal(ks[1], (E, 1), dtype=jnp.float32)
        src = jax.random.randint(ks[2], (E,), 0, N, dtype=jnp.int32)
        dst = jax.random.randint(ks[3], (E,), 0, N, dtype=jnp.int32)
        s_msg = 1.0 / np.sqrt(2 * H + 1)
        W_msg = jax.random.uniform(ks[4], (T, 2 * H, 2 * H + 1), jnp.float32, -s_msg, s_msg)
        b_msg = jax.random.uniform(ks[5], (T, 2 * H), jnp.float32, -s_msg, s_msg)
        s_gru = 1.0 / np.sqrt(H)
        W_ih = jax.random.uniform(ks[6], (T, 3 * H, 2 * H), jnp.float32, -s_gru, s_gru)
        W_hh = jax.random.uniform(ks[7], (T, 3 * H, H), jnp.float32, -s_gru, s_gru)
        b_ih = jax.random.uniform(ks[8], (T, 3 * H), jnp.float32, -s_gru, s_gru)
        b_hh = jax.random.uniform(ks[9], (T, 3 * H), jnp.float32, -s_gru, s_gru)
        return {'hv': hv, 'he': he, 'src': src, 'dst': dst, 'W_msg': W_msg, 'b_msg': b_msg, 'W_ih': W_ih, 'W_hh': W_hh, 'b_ih': b_ih, 'b_hh': b_hh}
    _L1_gnn_all = _L1_gnn_setup()
    _L1_gnn_in = {k: v for k, v in _L1_gnn_all.items() if k in ('W_msg', 'b_msg', 'W_ih', 'W_hh', 'b_ih', 'b_hh')}
    del _L1_gnn_all
    return {'x': x, 'src': src, 'dst': dst, 'edge_weight1': edge_weight1, 'L0_gnn_W': _L0_gnn_in['W'], 'L0_gnn_b': _L0_gnn_in['b'], 'L1_gnn_W_msg': _L1_gnn_in['W_msg'], 'L1_gnn_b_msg': _L1_gnn_in['b_msg'], 'L1_gnn_W_ih': _L1_gnn_in['W_ih'], 'L1_gnn_W_hh': _L1_gnn_in['W_hh'], 'L1_gnn_b_ih': _L1_gnn_in['b_ih'], 'L1_gnn_b_hh': _L1_gnn_in['b_hh']}

def reference(x, src, dst, edge_weight1, L0_gnn_W, L0_gnn_b, L1_gnn_W_msg, L1_gnn_b_msg, L1_gnn_W_ih, L1_gnn_W_hh, L1_gnn_b_ih, L1_gnn_b_hh):
    import jax
    import jax.numpy as jnp

    def _L0_gnn_ref(x, edge_index, W, b):
        import jax, jax.numpy as jnp
        import numpy as np
        N_NODES = 3125
        N_EDGES = 50000
        IN_FEAT = 64
        OUT_FEAT = 64
        row, col = (edge_index[0], edge_index[1])
        ones = jnp.ones((edge_index.shape[1],), dtype=x.dtype)
        deg = jax.ops.segment_sum(ones, row, num_segments=N_NODES)
        dis = jnp.where(deg > 0, jax.lax.rsqrt(jnp.maximum(deg, 1.0)), 0.0)
        w = -(dis[row] * dis[col])

        def prop(h):
            return jax.ops.segment_sum(w[:, None] * h[row], col, num_segments=N_NODES)
        tx0 = x
        tx1 = prop(x)
        out = tx0 @ W[0] + tx1 @ W[1] + b
        return jax.nn.relu(out)

    def _L1_gnn_ref(hv, he, src, dst, W_msg, b_msg, W_ih, W_hh, b_ih, b_hh):
        import jax, jax.numpy as jnp
        import numpy as np
        N = 3125
        E = 50000
        H = 64
        T = 2

        def gru_cell(x, h, W_ih_t, W_hh_t, b_ih_t, b_hh_t):
            gi = x @ W_ih_t.T + b_ih_t
            gh = h @ W_hh_t.T + b_hh_t
            ir, iz, inn = jnp.split(gi, 3, axis=1)
            hr, hz, hn = jnp.split(gh, 3, axis=1)
            r = jax.nn.sigmoid(ir + hr)
            z = jax.nn.sigmoid(iz + hz)
            n = jnp.tanh(inn + r * hn)
            return (1.0 - z) * n + z * h
        n_nodes = hv.shape[0]
        n_rounds = W_msg.shape[0]
        for t in range(n_rounds):
            feat = jnp.concatenate([hv[dst], hv[src], he], axis=1)
            act = feat @ W_msg[t].T + b_msg[t]
            a = jax.ops.segment_sum(act, dst, num_segments=n_nodes)
            hv = gru_cell(a, hv, W_ih[t], W_hh[t], b_ih[t], b_hh[t])
        return hv
    edge_index = jnp.stack([src, dst])
    h = jnp.maximum(_layernorm(x, axis=-1), 0.0)
    x = x + _L0_gnn_ref(h, edge_index, L0_gnn_W, L0_gnn_b)
    h = jnp.maximum(_layernorm(x, axis=-1), 0.0)
    x = x + _L1_gnn_ref(h, edge_weight1, src, dst, L1_gnn_W_msg, L1_gnn_b_msg, L1_gnn_W_ih, L1_gnn_W_hh, L1_gnn_b_ih, L1_gnn_b_hh)
    return x

_drawn_inputs = setup_inputs


def setup_inputs(seed=0):
    import zlib

    import numpy as np

    out = dict(_drawn_inputs(seed))
    spreads = {}
    factors = {'L1_gnn_b_hh': 2.81}
    for name, (base, spread) in spreads.items():
        noise = np.random.default_rng([zlib.crc32(name.encode()), seed]).standard_normal(out[name].shape)
        drawn = base * np.exp(spread * noise) if base else spread * noise
        out[name] = jnp.asarray(drawn.astype(out[name].dtype))
    for name, factor in factors.items():
        out[name] = (out[name] * factor).astype(out[name].dtype)
    return out
```

```python
import numpy as np
import concourse.bass as bass
import concourse.mybir as mybir
from concourse.alu_op_type import AluOpType as ALU

F32, BF16, FP16, I32 = mybir.dt.float32, mybir.dt.bfloat16, mybir.dt.float16, mybir.dt.int32
U32 = mybir.dt.uint32
ACT = mybir.ActivationFunctionType
AX = mybir.AxisListType

N, F, E = 3125, 64, 103125
P, NB = 125, 25
EROWS, EP = 125, 825
D = 13
SLOTS = 4
WCAP = 128 * SLOTS
KEYS = D * NB
KPAD = KEYS + 1
NPAIR = -(-N // (2 * D))
PAIRS = 4
TURNS = NPAIR // PAIRS
NW = 2 * NPAIR
NDIF = 5
DC = NW * D
NWT = 256
COUNT_MAX = 256
MAGIC = 1.5 * 2 ** 23
EPS = 1e-5
GROUPS = [range(0, 4), range(4, 8), range(8, 12), range(12, 16), range(16, 20), range(20, 23), range(23, 25)]
G, NG = 4, len(GROUPS)
PARTS = 3 * F
SLOT = 256
XW = F + 4
GATES = 4 * F
REC = 4
ACC = F + 2
PH_WORDS = 9010


def build_program(nc, x, src, dst, ew, w0, b0, wmsg, bmsg, wih, whh, bih, bhh, out):
    from contextlib import ExitStack
    ctx = ExitStack()
    sb = lambda name, shape, dt: ctx.enter_context(nc.sbuf_tensor(name, shape, dt))
    sem = lambda name: ctx.enter_context(nc.semaphore(name))

    recs = nc.dram_tensor("edge_records", (E * REC,), F32).ap()
    weight_sums = nc.dram_tensor("weight_sums", (3, DC * NB), F32).ap()
    feat_rows = nc.dram_tensor("feature_rows", (N, F), F32).ap()

    with ctx:
        counts = sb("counts", [128, NB, DC], BF16)
        xs = sb("xs", [P, NB, F], F32)
        state = sb("state", [P, NB, XW], F32)
        ident = sb("ident", [128, 128], F32)
        identb = sb("identb", [128, 128], BF16)
        w01 = sb("w01", [128, F], F32)
        bias0 = sb("bias0", [P, F], F32)
        wc1 = sb("wc1", [128, 2, 3 * F], F32)
        wc2 = sb("wc2", [XW, 2, GATES], F32)
        dis = sb("dis", [P, NB], F32)
        ndis = sb("ndis", [P, NB], F32)
        small = sb("small", [128, 64], F32)
        starts = sb("starts", [1, NWT], I32)
        flag_i = sb("flag_i", [1, 1], I32)
        phase = sb("phase", [128, PH_WORDS], F32)
        ps = ctx.enter_context(nc.psum_tensor("ps", [128, 8, 512], F32))

        class Carve:
            def __init__(self, flat, size):
                self.flat, self.at, self.size = flat, 0, size
            def __call__(self, words, parts=128, dt=F32):
                v = self.flat[0:parts, self.at:self.at + words]
                self.at += words
                assert self.at <= self.size, (self.at, self.size)
                return v if dt == F32 else v.bitcast(dt)

        flat = counts[:, :, :].rearrange("p a b -> p (a b)").bitcast(F32)
        e = Carve(flat, NB * DC // 2)
        dstx = e(EP + COUNT_MAX, dt=I32)
        srci = e(EP, dt=I32)
        wgt = e(EP)
        rec = e(EP * REC)
        key_b, key_q, tmp_a, tmp_b = e(EP), e(EP), e(EP), e(EP)
        he_hi, he_r = e(EP), e(EP)
        rows_i = e(2 * EP, dt=I32).rearrange("p (g n) -> p g n", g=2)
        rows_f = e(2 * EP).rearrange("p (g n) -> p g n", g=2)
        junk = e(2 * EP).rearrange("p (g n) -> p g n", g=2)
        wih_n = e(4 * 128, parts=96).rearrange("p (t g k) -> p t g k", t=2, g=2)
        whh_n = e(4 * F, parts=96).rearrange("p (t g k) -> p t g k", t=2, g=2)
        wmsg_n = e(2 * 130).rearrange("p (t k) -> p t k", t=2)
        wihT = e(2 * 3 * F).rearrange("p (t k) -> p t k", t=2)
        ln_a = e(NB * F, parts=P).rearrange("p (b f) -> p b f", f=F)
        ln_b = e(NB * F, parts=P).rearrange("p (b f) -> p b f", f=F)
        rec3 = rec.rearrange("p (n r) -> p n r", r=REC)
        rec16 = rec.bitcast(BF16).rearrange("p (n r) -> p n r", r=2 * REC)

        g_ = Carve(flat, NB * DC // 2)
        iota_n = g_(N, parts=P)
        hot_n = g_(N, parts=P)
        acc = g_(NB * ACC, parts=P).rearrange("p (b f) -> p b f", f=ACC)
        g_idx = g_(2, parts=P, dt=I32)
        g_idf, g_wgt = g_(1, parts=P), g_(1, parts=P)
        g_msg = g_(ACC, parts=P)
        g_rows = g_(NB * F, parts=P).rearrange("p (b f) -> p b f", f=F)

        b_ = Carve(phase[:, :], PH_WORDS)
        iota_k = b_(2 * KPAD // 2, dt=FP16).rearrange("p (w k) -> p w k", w=2)
        iota_s = b_(64, dt=FP16)
        record = b_(PAIRS * 2 * SLOTS * REC).rearrange("p (q w j r) -> p q w j r", q=PAIRS, w=2, r=REC)
        record16 = record.rearrange("p q w j r -> p (q w j r)").bitcast(BF16).rearrange(
            "p (q w j r) -> p q w j r", q=PAIRS, w=2, r=2 * REC)
        key = b_(2 * 2 * SLOTS).rearrange("p (h w j) -> p h w j", h=2, w=2)
        dif = b_(2 * NDIF * 64, dt=FP16).rearrange("p (h m k) -> p h m k", h=2, m=NDIF)
        hot_s = b_(2 * 2 * SLOTS * 64, dt=BF16).rearrange("p (h m k) -> p h m k", h=2, m=2 * SLOTS)
        hot_k = b_(2 * 2 * SLOTS * KPAD // 2, dt=BF16).rearrange("p (h m k) -> p h m k", h=2, m=2 * SLOTS)
        herows = b_(PAIRS * 2 * KEYS).rearrange("p (q w k) -> p q w k", q=PAIRS, w=2)
        pair_off = b_(NPAIR)
        zeros = b_((KEYS + 1) // 2 + 1, dt=BF16)

        r_ = Carve(phase[:, :], PH_WORDS)
        parts = [r_((NB * (PARTS + 1) + 1) // 2, dt=BF16)[:, 0:NB * (PARTS + 1)].rearrange(
            "p (b f) -> p b f", f=PARTS + 1) for _ in range(2)]
        x1 = [r_(G * 2 * F, parts=P).rearrange("p (b f) -> p b f", f=2 * F) for _ in range(2)]
        x2 = [r_(G * XW, parts=P).rearrange("p (b f) -> p b f", f=XW) for _ in range(2)]
        scaled = parts[1].rearrange("p b f -> p (b f)")[0:P, 0:2 * NB * F].bitcast(F32).rearrange("p (b f) -> p b f", f=F)
        wsums = phase[0:P, r_.at:r_.at + 3 * NB * NB].rearrange("p (k b c) -> p k b c", k=3, b=NB)
        assert 3 * NB * NB <= 4 * 2 * P + G * 4 * F
        xT = r_(4 * 2 * P).rearrange("p (b c n) -> p b c n", b=4, c=2)
        rz = r_(G * 2 * F, parts=P).rearrange("p (b f) -> p b f", f=2 * F)
        nn = r_(G * 2 * F, parts=P).rearrange("p (b f) -> p b f", f=2 * F)
        ua = r_(G * F, parts=P).rearrange("p (b f) -> p b f", f=F)
        ub = r_(G * F, parts=P).rearrange("p (b f) -> p b f", f=F)
        stat = r_(4 * G, parts=P).rearrange("p (k b) -> p k b", k=4)

        thr, cnt, rowi, rp = small[:, 0:2], small[:, 2:4], small[:, 4:6], small[:, 6:8]
        rowi_i, rowi_u = small[:, 8:10].bitcast(I32), small[:, 8:10].bitcast(U32)
        viol, dst0, ones_c = small[0:P, 10:11], small[0:P, 11:12], small[:, 12:13]
        flag_f, span = small[0:1, 14:15], small[0:1, 15:16]
        cnt2 = small[:, 16:18]
        rp_row = e(2 * NWT, parts=1)
        lns = sb("lns", [P, 4, NB], F32)

        ps_win = [ps[:, 2 * q:2 * q + 2, :] for q in range(2)]
        ps_deg, ps_misc = ps[:, 4, :], ps[:, 5, :]
        ps_iota = ps[:, 5, 0:P]
        ps_wt = [ps[:, 6, :], ps[:, 7, :]]
        ps_sum = [ps[:, 2 * k:2 * k + 2, :].rearrange("p a (c f) -> p (a c) f", f=SLOT) for k in range(2)]
        ps_T = [ps[:, 4 + k, :].rearrange("p (s n) -> p s n", s=4) for k in range(2)]
        ps_G = [ps[:, 6 + k, 0:GATES] for k in range(2)]

        tails_set = sem("tails_set")
        dst_in, src_in, wgt_in, x_in = sem("dst_in"), sem("src_in"), sem("wgt_in"), sem("x_in")
        weights_in = sem("weights_in")
        ids_made, tables_made = sem("ids_made"), sem("tables_made")
        dve = sem("dve_done")
        pool = sem("pool_done")
        actc = sem("act_done")
        pec = sem("pe_done")
        rowidx_ready, rows_in = sem("rowidx_ready"), [sem("rows_in0"), sem("rows_in1")]
        keys_made, parts_made = sem("keys_made"), sem("parts_made")
        records_out = sem("records_out")
        starts_ready = sem("starts_ready")
        record_in = [sem(f"record_in{q}") for q in range(PAIRS)]
        keys_ready = sem("keys_ready")
        iota_ready = sem("iota_ready")
        difs_ready = sem("difs_ready")
        hots_ready = sem("hots_ready")
        pair_summed = sem("pair_summed")
        pair_out = sem("pair_out")
        wsum_out = [sem(f"wsum_out{h}") for h in range(2)]
        wsum_in = sem("wsum_in")
        scaled_ready = sem("scaled_ready")
        rounded = sem("rounded")
        counted = sem("counted")
        state_ready = sem("state_ready")
        sums_ready = sem("sums_ready")
        x1_state, x1_ready = sem("x1_state"), sem("x1_ready")
        trans_done = sem("trans_done")
        trans_out = sem("trans_out")
        gates_done = sem("gates_done")
        gates_out = sem("gates_out")
        tanh_in, tanh_out = sem("tanh_in"), sem("tanh_out")
        var_in, std_out = sem("var_in"), sem("std_out")
        result_ready, stored = sem("result_ready"), sem("stored")
        g_tables, g_rows_out, g_in, g_gathered = sem("g_tables"), sem("g_rows_out"), sem("g_in"), sem("g_gathered")
        g_weighed = sem("g_weighed")
        g_hot, g_summed, g_added, g_feats = sem("g_hot"), sem("g_summed"), sem("g_added"), sem("g_feats")

        def chain_of(eng, s):
            count = [0]
            def link(ins, wait=True):
                count[0] += 1
                ins.then_inc(s, 1)
                if wait:
                    eng.wait_ge(s, count[0])
                return count[0]
            link.count = count
            return link

        dst_rows = dst.rearrange("(r n) -> r n", n=EP)
        src_rows = src.rearrange("(r n) -> r n", n=EP)
        wgt_rows = ew.rearrange("(r n) o -> r (n o)", n=EP)
        out_v = out.rearrange("(b p) f -> p b f", p=P)
        N_WEIGHTS = 2 + 2 * 7

        def out_count(t, k):
            if isinstance(k, int) and k < 0:
                return out_count(t - 1, k + NB)
            return k + 1 if t == 0 else NB + 2 * NB * (t - 1) + 2 * (k + 1)

        def blocks(g):
            return slice(GROUPS[g][0], GROUPS[g][-1] + 1)

        halves = [slice(0, 13), slice(13, NB)]

        at = {}

        block = ctx.enter_context(nc.Block())

        @block.vector
        def _(v):
            link = chain_of(v, dve)
            tt, ts, stt = nc.vector.tensor_tensor, nc.vector.tensor_scalar, nc.vector.scalar_tensor_tensor
            red = nc.vector.tensor_reduce

            nc.vector.memset(dstx[96:128, EP:], 1 << 20).then_inc(tails_set, 1)
            nc.vector.memset(zeros, 0.0).then_inc(tails_set, 1)
            nc.vector.memset(wc2[:, :, :], 0.0).then_inc(tails_set, 1)
            nc.vector.memset(ones_c, 1.0).then_inc(tails_set, 1)

            v.wait_ge(dst_in, 48)
            link(nc.vector.tensor_copy(dst0, dstx[0:P, 0:1]))
            at["dst0"] = link.count[0]
            v.wait_ge(pec, 1)
            v.wait_ge(tables_made, 4)
            for g in range(2):
                link(ts(junk[:, g, 0:P], ps_misc[:, 0:P], thr[:, g:g + 1], 0.0, ALU.is_lt, ALU.add,
                        accum_out=cnt[:, g:g + 1]))
            link(ts(rowi, cnt, -1.0, 0.0, ALU.add, ALU.max))
            nc.vector.tensor_copy(rowi_i, rowi).then_inc(rowidx_ready, 1)
            link(tt(tmp_a[0:P], dstx[0:P, 1:EP + 1], dstx[0:P, 0:EP], ALU.is_lt))
            link(tt(tmp_b[0:P], dstx[0:P, COUNT_MAX:COUNT_MAX + EP], dstx[0:P, 0:EP], ALU.is_equal))
            link(tt(tmp_a[0:P], tmp_a[0:P], tmp_b[0:P], ALU.add))
            link(red(viol, tmp_a[0:P], AX.X, ALU.add))
            at["viol"] = link.count[0]

            v.wait_ge(src_in, 16)
            link(ts(key_q[0:P], srci[0:P], 1.0 / P, -0.5 + 0.5 / P, ALU.mult, ALU.add))
            link(ts(key_b[0:P], key_q[0:P], MAGIC, -MAGIC, ALU.add, ALU.add))
            stt(rec3[0:P, :, 1], key_b[0:P], -float(P), srci[0:P], ALU.mult, ALU.add).then_inc(keys_made, 1)
            stt(rec3[0:P, :, 0], dstx[0:P, 0:EP], float(NB), key_b[0:P], ALU.mult, ALU.add).then_inc(keys_made, 1)

            for g in range(2):
                v.wait_ge(rows_in[g], 16)
                link(nc.vector.tensor_copy(rows_f[:, g, :], rows_i[:, g, :]))
                link(ts(junk[:, g, :], rows_f[:, g, :], thr[:, g:g + 1], 0.0, ALU.is_lt, ALU.add,
                        accum_out=cnt2[:, g:g + 1]))
            link(stt(rp, rowi, float(EP), cnt2, ALU.mult, ALU.add))
            at["rp"] = link.count[0]
            v.wait_ge(pec, 3)
            link(nc.vector.tensor_copy(rp_row[0:1, 0:NWT], ps_misc[0:1, 128:128 + NWT]))
            link(ts(rp_row[0:1, NWT:], rp_row[0:1, 0:NWT], float(E - WCAP), None, ALU.min))
            ts(starts[0:1, :], rp_row[0:1, NWT:], float(REC), None, ALU.mult).then_inc(starts_ready, 1)
            link(tt(rp_row[0:1, 0:NWT - 1], rp_row[0:1, 1:NWT], rp_row[0:1, NWT:2 * NWT - 1], ALU.subtract))
            link(red(span, rp_row[0:1, 0:NWT - 1], AX.X, ALU.max))
            link(ts(span, span, float(WCAP), None, ALU.is_gt))
            link(tt(flag_f, span, ps_misc[0:1, 400:401], ALU.add))
            link(ts(flag_f, flag_f, 1.0, None, ALU.min))
            nc.vector.tensor_copy(flag_i[0:1, :], flag_f).then_inc(starts_ready, 1)

            for t in range(2):
                v.wait_ge(pec, 4 + 2 * t)
                link(nc.vector.tensor_copy(wihT[:, t, :], ps_wt[t][:, 0:3 * F]))
                link(nc.vector.tensor_copy(wc2[0:F, t, 0:2 * F], ps_wt[t][0:F, 192:320]))
                link(nc.vector.tensor_copy(wc2[0:F, t, 3 * F:], ps_wt[t][0:F, 320:384]))
                at["wihT", t] = link.count[0]
                v.wait_ge(pec, 5 + 2 * t)
                link(nc.vector.tensor_copy(wc1[:, t, :], ps_wt[t][:, 0:3 * F]))
                link(nc.vector.tensor_copy(wc2[F:F + 2, t, 0:3 * F], ps_wt[t][F:F + 2, 192:384]))
            at["wc"] = link.count[0]

            v.wait_ge(x_in, 16)
            bc = lambda a, n=NB: a.unsqueeze(2).broadcast_to([P, n, F])
            link(red(lns[:, 0, :], xs[:, :, :], AX.X, ALU.add))
            link(ts(lns[:, 1, :], lns[:, 0, :], 1.0 / F, None, ALU.mult))
            link(tt(ln_a, xs[:, :, :], bc(lns[:, 1, :]), ALU.subtract))
            link(tt(ln_b, ln_a, ln_a, ALU.mult))
            link(red(lns[:, 2, :], ln_b, AX.X, ALU.add))
            link(ts(lns[:, 2, :], lns[:, 2, :], 1.0 / F, EPS, ALU.mult, ALU.add))
            at["var0"] = link.count[0]
            v.wait_ge(actc, 1)
            link(nc.vector.reciprocal(lns[:, 0, :], lns[:, 3, :]))
            link(stt(state[:, :, 0:F], ln_a, 0.0, bc(lns[:, 0, :]), ALU.max, ALU.mult))
            link(nc.vector.memset(state[:, :, F + 2:], 1.0))
            at["state0"] = link.count[0]

            v.wait_ge(starts_ready, 2)
            general = v.value_load(flag_i[0:1, 0:1], min_val=0, max_val=1)

            def write_parts(to, gb, source, a):
                hi, mid, lo = (parts[to][0:P, gb, k * F:(k + 1) * F] for k in range(3))
                link(nc.vector.tensor_copy(hi, source))
                link(tt(a, source, hi, ALU.subtract))
                link(nc.vector.tensor_copy(mid, a))
                return tt(lo, a, mid, ALU.subtract)

            def scale_by_degree(fast):
                link(ts(lns[:, 1, :], lns[:, 0, :], 1.0, None, ALU.max))
                link(ts(lns[:, 2, :], lns[:, 0, :], 1.0, None, ALU.min))
                at["degree", fast] = link.count[0]
                v.wait_ge(actc, 2)
                link(nc.vector.reciprocal(dis[:, :], lns[:, 3, :]))
                link(tt(dis[:, :], dis[:, :], lns[:, 2, :], ALU.mult))
                link(ts(ndis[:, :], dis[:, :], -1.0, None, ALU.mult))
                if fast:
                    link(nc.vector.memset(parts[0][0:P, :, PARTS:], 1.0))
                if not fast:
                    link(tt(g_rows, state[:, :, 0:F], bc(dis[:, :]), ALU.mult))
                    at["features", fast] = link.count[0]
                    return
                for c in range(2):
                    gb = halves[c]
                    tt(scaled[:, gb], state[:, gb, 0:F], bc(dis[:, gb], gb.stop - gb.start), ALU.mult).then_inc(scaled_ready, 1)
                for k in (1, 2):
                    for c in range(2):
                        gb = halves[c]
                        v.wait_ge(rounded, 2 * (k - 1) + c + 1)
                        taken = parts[0][0:P, gb, (k - 1) * F:k * F]
                        if k == 1:
                            tt(scaled[:, gb], scaled[:, gb], taken, ALU.subtract).then_inc(scaled_ready, 1)
                        else:
                            link(tt(parts[0][0:P, gb, 2 * F:PARTS], scaled[:, gb], taken, ALU.subtract))
                            at["features", fast, c] = link.count[0]
                at["features", fast] = link.count[0]

            def gathered_sums(k, index, width):
                link(nc.vector.memset(acc[:, :, :], 0.0))
                with v.Fori(0, EP) as r:
                    v.wait_ge(g_in, 48 * (k * EP + r + 1))
                    nc.vector.tensor_copy(g_idf, g_idx[:, index:index + 1]).then_inc(g_hot, 1)
                    v.wait_ge(g_hot, 2 * (k * EP + r) + 1)
                    ts(hot_n, iota_n, g_idf, None, ALU.is_equal).then_inc(g_hot, 1)
                    v.wait_ge(g_summed, k * EP + r + 1)
                    for b in range(4):
                        n = min(7, NB - 7 * b)
                        a = acc[:, 7 * b:7 * b + n, 0:width]
                        s = ps[0:P, b, 0:7 * ACC].rearrange("p (s f) -> p s f", f=ACC)[:, 0:n, 0:width]
                        tt(a, a, s, ALU.add).then_inc(g_added, 1)
                    v.wait_ge(g_added, 4 * (k * EP + r + 1))

            def sums_to_x1(t, g, fast):
                gb, n, K = blocks(g), len(GROUPS[g]), t * NG + g
                x = x1[K % 2][:, 0:n, F:]
                v.wait_ge(x1_state, K + 1)
                if fast:
                    v.wait_ge(sums_ready, K + 1)
                    s = ps_sum[K % 2]
                    u = ua[:, 0:n]
                    i = red(u if t == 0 else x, s[0:P, 0:n, 0:PARTS].rearrange("p b (k f) -> p b f k", k=3),
                            AX.X, ALU.add)
                    if t > 0:
                        i.then_inc(x1_ready, 1)
                        return
                    link(i)
                    link(nc.vector.tensor_copy(state[:, gb, F + 1:F + 2], s[0:P, 0:n, PARTS:PARTS + 1]))
                    tt(x, u, bc(ndis[:, gb], n), ALU.mult).then_inc(x1_ready, 1)
                elif t > 0:
                    nc.vector.tensor_copy(x, acc[:, gb, 0:F]).then_inc(x1_ready, 1)
                else:
                    link(nc.vector.tensor_copy(state[:, gb, F + 1:F + 2], acc[:, gb, F:F + 1]))
                    link(nc.vector.tensor_copy(state[:, gb, F:F + 1], acc[:, gb, F + 1:F + 2]))
                    tt(x, acc[:, gb, 0:F], bc(ndis[:, gb], n), ALU.mult).then_inc(x1_ready, 1)

            def finish_first(g):
                gb, n = blocks(g), len(GROUPS[g])
                v.wait_ge(gates_out, out_count(0, GROUPS[g][-1]))
                bias = bias0[:, :].unsqueeze(1).broadcast_to([P, n, F])
                a, b, st = ua[:, 0:n], ub[:, 0:n], stat[:, :, 0:n]
                link(tt(a, nn[:, 0:n, 0:F], bias, ALU.add))
                link(stt(xs[:, gb, :], a, 0.0, xs[:, gb, :], ALU.max, ALU.add))
                link(red(st[:, 0, :], xs[:, gb, :], AX.X, ALU.add))
                link(ts(st[:, 1, :], st[:, 0, :], 1.0 / F, None, ALU.mult))
                link(tt(a, xs[:, gb, :], bc(st[:, 1, :], n), ALU.subtract))
                link(tt(b, a, a, ALU.mult))
                link(red(st[:, 2, :], b, AX.X, ALU.add))
                ts(st[:, 2, :], st[:, 2, :], 1.0 / F, EPS, ALU.mult, ALU.add).then_inc(var_in, 1)
                v.wait_ge(std_out, g + 1)
                link(nc.vector.reciprocal(st[:, 0, :], st[:, 3, :]))
                return stt(state[:, gb, 0:F], a, 0.0, bc(st[:, 0, :], n), ALU.max, ALU.mult)

            def finish_gru(t, g):
                gb, n = blocks(g), len(GROUPS[g])
                v.wait_ge(gates_out, out_count(t, GROUPS[g][-1]))
                a, b = ua[:, 0:n], ub[:, 0:n]
                link(tt(a, rz[:, 0:n, 0:F], nn[:, 0:n, F:], ALU.mult))
                tt(a, a, nn[:, 0:n, 0:F], ALU.add).then_inc(tanh_in, 1)
                v.wait_ge(tanh_out, (t - 1) * NG + g + 1)
                link(tt(a, state[:, gb, 0:F], b, ALU.subtract))
                link(tt(a, a, rz[:, 0:n, F:], ALU.mult))
                return tt(state[:, gb, 0:F], a, b, ALU.add)

            def rounds(t, fast):
                if t == 0 and fast:
                    v.wait_ge(wsum_in, 48)
                    link(red(state[:, :, F:F + 1], wsums.rearrange("p k b c -> p b k c"), AX.XY, ALU.add))
                for g in range(NG + 1):
                    if g < NG:
                        sums_to_x1(t, g, fast)
                    if g == 0:
                        continue
                    gb = blocks(g - 1)
                    i = finish_first(g - 1) if t == 0 else finish_gru(t, g - 1)
                    if t == 2:
                        link(i)
                        tt(xs[:, gb, :], state[:, gb, 0:F], xs[:, gb, :], ALU.add).then_inc(result_ready, 1)
                    elif fast:
                        link(i)
                        i = write_parts((t + 1) % 2, gb, state[:, gb, 0:F], ua[:, 0:len(GROUPS[g - 1])])
                    else:
                        link(i)
                        i = nc.vector.tensor_copy(g_rows[:, gb, :], state[:, gb, 0:F])
                    if t < 2:
                        i.then_inc(state_ready, 1)
                        v.wait_ge(state_ready, t * NG + g)

            base = link.count[0]

            with v.If(general == 0):
                def one_hots(p, q):
                    h = q % 2
                    v.wait_ge(keys_ready, 2 * (p + 1))
                    for m in range(2 * SLOTS):
                        w, j = m // SLOTS, m % SLOTS
                        ts(hot_k[:, h, m, 0:KEYS], iota_k[:, w, 0:KEYS], key[:, h, w, j:j + 1], None, ALU.is_equal)
                        if m >= NDIF:
                            ts(hot_s[:, h, m, 0:P], iota_s[:, 0:P], record[:, q, w, j, 1:2], None, ALU.is_equal)
                    v.wait_ge(difs_ready, p + 1)
                    ts(hot_s[:, h, 0:NDIF, 0:P], dif[:, h, :, 0:P], 0.0, None, ALU.is_equal).then_inc(hots_ready, 1)

                with v.Fori(0, TURNS) as i:
                    for q in range(PAIRS):
                        one_hots(PAIRS * i + q, q)
                for p in range(PAIRS * TURNS, NPAIR):
                    one_hots(p, p % PAIRS)
                v.wait_ge(counted, 1)
                link(red(lns[:, 0, :], ps_deg[0:P, 0:KEYS].rearrange("p (b d) -> p b d", d=D), AX.X, ALU.add))
                scale_by_degree(True)
                for t in range(3):
                    rounds(t, True)
            link.count[0] = base
            with v.Else():
                v.wait_ge(records_out, 32)
                link(nc.vector.memset(g_msg, 1.0))
                at["ones"] = link.count[0]
                v.wait_ge(g_tables, 1)
                gathered_sums(0, 1, 1)
                link(nc.vector.tensor_copy(lns[:, 0, :].unsqueeze(2), acc[:, :, 0:1]))
                scale_by_degree(False)
                for t in range(3):
                    gathered_sums(t + 1, 0, ACC)
                    rounds(t, False)

        @block.gpsimd
        def _(g):
            link = chain_of(g, pool)
            gp = nc.gpsimd
            link(gp.memset(ident[:, :], 0.0))
            link(gp.affine_select(out=ident[:, :], in_=ident[:, :], compare_op=ALU.not_equal, fill=1.0, base=0,
                                  pattern=[[-1, 128]], channel_multiplier=1))
            gp.tensor_copy(identb[:, :], ident[:, :]).then_inc(ids_made, 1)
            gp.iota(thr, [[128 * D, 2]], base=0, channel_multiplier=D, allow_small_or_imprecise_dtypes=True).then_inc(tables_made, 1)
            gp.iota(iota_s, [[1, 128]], base=0, channel_multiplier=0, allow_small_or_imprecise_dtypes=True).then_inc(tables_made, 1)
            gp.iota(iota_k, [[KEYS, 2], [1, KPAD]], base=0, channel_multiplier=0,
                    allow_small_or_imprecise_dtypes=True).then_inc(tables_made, 1)
            gp.iota(pair_off, [[2 * KEYS, NPAIR]], base=0, channel_multiplier=0,
                    allow_small_or_imprecise_dtypes=True).then_inc(tables_made, 1)
            g.wait_ge(wgt_in, 16)
            hi, mid, lo = (rec16[0:P, :, 4 + k] for k in range(3))
            link(gp.tensor_copy(hi, wgt[0:P]))
            link(gp.tensor_tensor(he_r[0:P], wgt[0:P], hi, ALU.subtract))
            link(gp.tensor_copy(mid, he_r[0:P]))
            gp.memset(rec16[0:P, :, 7], 0.0).then_inc(parts_made, 1)
            gp.tensor_tensor(lo, he_r[0:P], mid, ALU.subtract).then_inc(parts_made, 1)

            g.wait_ge(rowidx_ready, 1)
            for k in range(2):
                gp.indirect_dma_start(rows_i[:, k, :], None, dst_rows,
                                      bass.IndirectOffsetOnAxis(ap=rowi_u[:, k:k + 1], axis=0)).then_inc(rows_in[k], 16)

            g.wait_ge(starts_ready, 2)
            general = g.value_load(flag_i[0:1, 0:1], min_val=0, max_val=1)

            def x1_state_half(t, n):
                gb, size, K = blocks(n), len(GROUPS[n]), t * NG + n
                if t > 0:
                    g.wait_ge(state_ready, (t - 1) * NG + n + 1)
                if K >= 2:
                    g.wait_ge(trans_done, NB * ((K - 2) // NG) + GROUPS[(K - 2) % NG][-1] + 1)
                if t == 0:
                    gp.tensor_copy(x1[K % 2][:, 0:size, 0:F], state[:, gb, 0:F]).then_inc(x1_state, 1)
                else:
                    link(gp.tensor_copy(x2[K % 2][:, 0:size], state[:, gb, :]))
                    gp.tensor_tensor(x1[K % 2][:, 0:size, 0:F], state[:, gb, 0:F],
                                     state[:, gb, F + 1:F + 2].broadcast_to([P, size, F]), ALU.mult).then_inc(x1_state, 1)

            base = link.count[0]
            with g.If(general == 0):
                def take(i, q, first=False):
                    p, h = PAIRS * i + q, q % 2
                    g.wait_ge(tables_made, 4)
                    g.wait_ge(record_in[q], 32 * (i + 1))
                    if not first:
                        g.wait_ge(pair_summed, p - 1)
                    gp.tensor_tensor(key[:, h].rearrange("p w j -> p (w j)"),
                                     record[:, q, :, :, 0].rearrange("p w j -> p (w j)"),
                                     pair_off[:, bass.ds(p, 1)].broadcast_to([128, 2 * SLOTS]),
                                     ALU.subtract).then_inc(keys_ready, 1)
                    gp.tensor_copy(hot_s[:, h, :, P:].rearrange("p (w j) k -> p w j k", w=2),
                                   record16[:, q, :, :, 4:7]).then_inc(keys_ready, 1)

                for q in range(PAIRS):
                    take(0, q, first=q < 2)
                with g.Fori(1, TURNS) as i:
                    for q in range(PAIRS):
                        take(i, q)
                for p in range(PAIRS * TURNS, NPAIR):
                    take(p // PAIRS, p % PAIRS)
                g.wait_ge(dve, at["features", True])
                for t in range(3):
                    for n in range(NG):
                        x1_state_half(t, n)
            link.count[0] = base
            with g.Else():
                g.wait_ge(dve, at["ones"])
                gp.iota(iota_n, [[1, N]], base=0, channel_multiplier=0,
                        allow_small_or_imprecise_dtypes=True).then_inc(g_tables, 1)
                for t in range(3):
                    with g.Fori(0, EP) as r:
                        g.wait_ge(g_in, 48 * ((t + 1) * EP + r + 1))
                        gp.tensor_tensor(g_msg[:, F + 1:], g_wgt, g_msg[:, F:F + 1], ALU.mult).then_inc(g_weighed, 1)
                        g.wait_ge(g_rows_out, 16 * (t + 1))
                        gp.indirect_dma_start(g_msg[:, 0:F], None, feat_rows,
                                              bass.IndirectOffsetOnAxis(ap=g_idx[:, 1:2].bitcast(U32), axis=0)
                                              ).then_inc(g_gathered, 16)
                        g.wait_ge(g_gathered, 16 * (t * EP + r + 1))
                    for n in range(NG):
                        x1_state_half(t, n)

        @block.scalar
        def _(a):
            act = nc.scalar.activation
            a.wait_ge(dve, at["var0"])
            act(lns[:, 3, :], lns[:, 2, :], ACT.Sqrt).then_inc(actc, 1)
            a.wait_ge(starts_ready, 2)
            general = a.value_load(flag_i[0:1, 0:1], min_val=0, max_val=1)

            def transposes_out(t, k):
                K = t * NB + k
                a.wait_ge(trans_done, K + 1)
                if K >= 4:
                    a.wait_ge(gates_done, K - 3)
                nc.scalar.copy(xT[:, K % 4, 0, :], ps_T[K % 2][:, 0, 0:P]).then_inc(trans_out, 1)
                if t > 0:
                    nc.scalar.copy(xT[0:XW, K % 4, 1, :], ps_T[K % 2][0:XW, 1, 0:P]).then_inc(trans_out, 1)

            def gates_to_sbuf(t, g, k):
                n, K = k - GROUPS[g][0], t * NB + k
                a.wait_ge(gates_done, K + 1)
                if n == 0 and t * NG + g > 0:
                    if t < 2 or g == 0:
                        a.wait_ge(state_ready, t * NG + g)
                    else:
                        a.wait_ge(result_ready, g)
                if t == 0:
                    nc.scalar.copy(nn[:, n, 0:F], ps_G[K % 2][0:P, 0:F]).then_inc(gates_out, 1)
                else:
                    act(rz[:, n, :], ps_G[K % 2][0:P, 0:2 * F], ACT.Sigmoid).then_inc(gates_out, 1)
                    nc.scalar.copy(nn[:, n, :], ps_G[K % 2][0:P, 2 * F:]).then_inc(gates_out, 1)

            def group_function(t, g):
                n = len(GROUPS[g])
                if t == 0:
                    a.wait_ge(var_in, g + 1)
                    act(stat[:, 3, 0:n], stat[:, 2, 0:n], ACT.Sqrt).then_inc(std_out, 1)
                else:
                    a.wait_ge(tanh_in, (t - 1) * NG + g + 1)
                    act(ub[:, 0:n], ua[:, 0:n], ACT.Tanh).then_inc(tanh_out, 1)

            def rounds(fast):
                a.wait_ge(dve, at["degree", fast])
                act(lns[:, 3, :], lns[:, 1, :], ACT.Sqrt).then_inc(actc, 1)
                if fast:
                    for k in range(2):
                        for c in range(2):
                            a.wait_ge(scaled_ready, 2 * k + c + 1)
                            act(parts[0][0:P, halves[c], k * F:(k + 1) * F], scaled[:, halves[c]], ACT.Copy).then_inc(rounded, 1)
                for t in range(3):
                    for g in range(NG):
                        for n, k in enumerate(GROUPS[g]):
                            transposes_out(t, k)
                            if k > 0:
                                last = GROUPS[g - (n == 0)][-1]
                                gates_to_sbuf(t, g - (n == 0), k - 1)
                                if k - 1 == last:
                                    group_function(t, g - 1)
                    gates_to_sbuf(t, NG - 1, NB - 1)
                    group_function(t, NG - 1)

            with a.If(general == 0):
                a.wait_ge(tables_made, 4)
                act(ps_iota, iota_s[:, 0:P], ACT.Copy).then_inc(iota_ready, 1)
                a.wait_ge(iota_ready, 1)

                def differences(i, q, first=False):
                    p = PAIRS * i + q
                    a.wait_ge(record_in[q], 32 * (i + 1))
                    if not first:
                        a.wait_ge(hots_ready, p - 1)
                    for m in range(NDIF):
                        i_ = act(dif[:, q % 2, m, 0:P], ps_iota, ACT.Identity,
                                 bias=record[:, q, m // SLOTS, m % SLOTS, 1:2], scale=-1.0)
                    i_.then_inc(difs_ready, 1)

                def evacuate(i, q, first=False):
                    p, h = PAIRS * i + q, q % 2
                    a.wait_ge(pair_summed, p + 1)
                    act(counts[:, :, bass.ds(p * 2 * D, 2 * D)].rearrange("p b (w d) -> p w b d", w=2),
                        ps_win[h][:, :, 0:KEYS].rearrange("p w (d b) -> p w b d", d=D), ACT.Copy).then_inc(pair_out, 1)
                    if not first:
                        a.wait_ge(wsum_out[q // 2], 16 * i)
                    act(herows[96:128, q, :, :], ps_win[h][96:128, :, 0:KEYS], ACT.Copy).then_inc(pair_out, 1)

                differences(0, 0, first=True)
                for q in range(PAIRS):
                    differences((q + 1) // PAIRS, (q + 1) % PAIRS, first=q == 0)
                    evacuate(0, q, first=True)
                with a.Fori(1, TURNS) as i:
                    for q in range(PAIRS):
                        differences(i + (q + 1) // PAIRS, (q + 1) % PAIRS)
                        evacuate(i, q)
                for p in range(PAIRS * TURNS, NPAIR):
                    if p + 1 < NPAIR:
                        differences((p + 1) // PAIRS, (p + 1) % PAIRS)
                    evacuate(p // PAIRS, p % PAIRS)
                rounds(True)
            with a.Else():
                rounds(False)

        @block.tensor
        def _(pe):
            mm = nc.tensor.matmul
            pe.wait_ge(ids_made, 1)
            pe.wait_ge(dve, at["dst0"])
            mm(ps_misc[:, 0:P], dst0.broadcast_to([P, 128]), ident[0:P, 0:P], start=True, stop=True).then_inc(pec, 1)
            pe.wait_ge(dve, at["rp"])
            for k in range(2):
                last = mm(ps_misc[0:1, 128 * (k + 1):128 * (k + 2)], rp[:, k:k + 1], ident[:, :], start=True, stop=True)
            last.then_inc(pec, 1)
            pe.wait_ge(tails_set, 4)
            mm(ps_misc[0:1, 400:401], viol, ones_c[0:P], start=True, stop=True).then_inc(pec, 1)
            pe.wait_ge(weights_in, 16 * N_WEIGHTS)
            for t in range(2):
                for k in range(2):
                    nc.tensor.transpose(ps_wt[t][:, 96 * k:96 * (k + 1)], wih_n[:, t, k, :], ident[0:96, 0:96])
                    last = nc.tensor.transpose(ps_wt[t][0:F, 192 + 96 * k:192 + 96 * (k + 1)], whh_n[:, t, k, :],
                                               ident[0:96, 0:96])
                last.then_inc(pec, 1)
                pe.wait_ge(dve, at["wihT", t])
                mm(ps_wt[t][:, 0:3 * F], wmsg_n[:, t, 0:2 * F], wihT[:, t, :], start=True, stop=True)
                mm(ps_wt[t][F:F + 2, 192:384], wmsg_n[:, t, 2 * F:], wihT[:, t, :], start=True, stop=True).then_inc(pec, 1)
            pe.wait_ge(starts_ready, 2)
            general = pe.value_load(flag_i[0:1, 0:1], min_val=0, max_val=1)

            def after_block(s, t, k):
                if not (t == 0 and k < 0):
                    pe.wait_ge(s, out_count(t, k))

            def transpose_block(t, k):
                g = [k in blocks_of for blocks_of in GROUPS].index(True)
                n, K = k - GROUPS[g][0], t * NG + g
                if n == 0:
                    pe.wait_ge(x1_ready, K + 1)
                after_block(trans_out, t, k - 2)
                into = ps_T[(t * NB + k) % 2]
                i = nc.tensor.transpose(into[:, 0, 0:P], x1[K % 2][:, n, :], ident[0:P, 0:P])
                if t > 0:
                    i = nc.tensor.transpose(into[0:XW, 1, 0:P], x2[K % 2][:, n, :], ident[0:P, 0:P])
                i.then_inc(trans_done, 1)

            def gates_block(t, k):
                pe.wait_ge(trans_out, out_count(t, k))
                after_block(gates_out, t, k - 2)
                K = t * NB + k
                o, x = ps_G[K % 2][0:P, :], xT[:, K % 4]
                if t == 0:
                    mm(o[:, 0:F], x[:, 0, :], w01[:, :], start=True, stop=True).then_inc(gates_done, 1)
                else:
                    mm(o, x[0:XW, 1, :], wc2[:, t - 1, :], start=True, stop=False, skip_group_check=True)
                    mm(o[:, 0:3 * F], x[:, 0, :], wc1[:, t - 1, :], start=False, stop=True,
                       skip_group_check=True).then_inc(gates_done, 1)

            def step(t, k):
                transpose_block(t, k)
                if k > 0:
                    gates_block(t, k - 1)

            def sums(t, g, k, sources):
                n, width = k - GROUPS[g][0], PARTS + 1 if t == 0 else PARTS
                for s in sources:
                    last = mm(ps_sum[(t * NG + g) % 2][:, n, 0:width], counts[0:P, s, k * P:k * P + 128],
                              parts[t % 2][0:P, s, 0:width], start=(s == 0 and n % 2 == 0), stop=(s == NB - 1),
                              skip_group_check=True)
                if k == GROUPS[g][-1] and sources[-1] == NB - 1:
                    last.then_inc(sums_ready, 1)

            def first_group(t):
                if t > 0:
                    pe.wait_ge(x1_ready, t * NG - 1)
                    pe.wait_ge(state_ready, t * NG - 2)
                else:
                    pe.wait_ge(dve, at["features", True, 0])
                known = range(0, GROUPS[NG - 2][0]) if t > 0 else range(0, halves[1].start)
                tail = GROUPS[NG - 1]
                for n, k in enumerate(GROUPS[0]):
                    sums(t, 0, k, known)
                    if t > 0 and n < len(tail):
                        step(t - 1, tail[n])
                    if t > 0 and n == len(tail):
                        gates_block(t - 1, NB - 1)
                if t == 0:
                    pe.wait_ge(dve, at["features", True])
                    for k in GROUPS[0]:
                        sums(t, 0, k, range(halves[1].start, NB))
                    return
                for g in (NG - 2, NG - 1):
                    pe.wait_ge(state_ready, (t - 1) * NG + g + 1)
                    for k in GROUPS[0]:
                        sums(t, 0, k, GROUPS[g])

            def other_group(t, g):
                if t * NG + g >= 2:
                    pe.wait_ge(x1_ready, t * NG + g - 1)
                before = GROUPS[g - 1]
                for n, k in enumerate(GROUPS[g]):
                    sums(t, g, k, range(NB))
                    if n < len(before):
                        step(t, before[n])
                for k in before[len(GROUPS[g]):]:
                    step(t, k)

            with pe.If(general == 0):
                pe.wait_ge(tails_set, 4)
                mm(ps_deg[:, 0:KEYS], identb[:, :], zeros[:, 0:KEYS], start=True, stop=False, skip_group_check=True)

                def degrees(p):
                    pe.wait_ge(pair_out, 2 * p + 1)
                    for w in range(2):
                        mm(ps_deg[:, 0:KEYS].rearrange("p (b d) -> p b d", d=D), identb[:, :],
                           counts[:, :, bass.ds((2 * p + w) * D, D)], start=False, stop=False, skip_group_check=True)

                def pair(p, q, first=False):
                    h = q % 2
                    pe.wait_ge(hots_ready, p + 1)
                    if not first:
                        pe.wait_ge(pair_out, 2 * (p - 1))
                    for m in range(2 * SLOTS):
                        last = mm(ps_win[h][:, m // SLOTS, 0:KEYS], hot_s[:, h, m, :], hot_k[:, h, m, 0:KEYS],
                                  start=(m % SLOTS == 0), stop=(m % SLOTS == SLOTS - 1))
                    last.then_inc(pair_summed, 1)

                for p in range(PAIRS):
                    pair(p, p, first=p < 2)
                    if p >= 2:
                        degrees(p - 2)
                with pe.Fori(1, TURNS) as i:
                    for q in range(PAIRS):
                        pair(PAIRS * i + q, q)
                        degrees(PAIRS * i + q - 2)
                for p in range(PAIRS * TURNS, NPAIR):
                    pair(p, p % PAIRS)
                    degrees(p - 2)
                degrees(NPAIR - 2)
                degrees(NPAIR - 1)
                mm(ps_deg[:, 0:KEYS], identb[:, :], zeros[:, 0:KEYS], start=False, stop=True,
                   skip_group_check=True).then_inc(counted, 1)
                for t in range(3):
                    first_group(t)
                    for g in range(1, NG):
                        other_group(t, g)
                for k in GROUPS[NG - 1]:
                    step(2, k)
                gates_block(2, NB - 1)
            with pe.Else():
                def gathered_sums(k, width):
                    with pe.Fori(0, EP) as r:
                        pe.wait_ge(g_hot, 2 * (k * EP + r + 1))
                        pe.wait_ge(g_in, 48 * (k * EP + r + 1))
                        if k > 0:
                            pe.wait_ge(g_weighed, (k - 1) * EP + r + 1)
                            pe.wait_ge(g_gathered, 16 * ((k - 1) * EP + r + 1))
                        for b in range(NB):
                            last = mm(ps[0:P, b // 7, ACC * (b % 7):ACC * (b % 7) + width], hot_n[:, b * P:(b + 1) * P],
                                      g_msg[:, 0:width], start=True, stop=True)
                        last.then_inc(g_summed, 1)
                gathered_sums(0, 1)
                for t in range(3):
                    gathered_sums(t + 1, ACC)
                    for k in range(NB):
                        step(t, k)
                    gates_block(t, NB - 1)

        @block.sync
        def _(sp):
            sp.wait_ge(tails_set, 1)
            def over(lo, hi):
                return bass.AP(dst.tensor, lo * EP, [[EP, hi - lo], [1, EP + COUNT_MAX]])
            sp.dma_start(dstx[0:112], over(0, 112)).then_inc(dst_in, 16)
            sp.dma_start(dstx[112:EROWS - 1], over(112, EROWS - 1)).then_inc(dst_in, 16)
            sp.dma_start(dstx[EROWS - 1:EROWS, 0:EP], dst_rows[EROWS - 1:EROWS, :]).then_inc(dst_in, 16)
            sp.dma_start(srci[0:P], src_rows).then_inc(src_in, 16)
            sp.dma_start(wgt[0:P], wgt_rows).then_inc(wgt_in, 16)
            sp.dma_start(xs[:, :, :], x.rearrange("(b p) f -> p b f", p=P)).then_inc(x_in, 16)
            sp.dma_start(w01[:, :], w0.rearrange("k i o -> (k i) o")).then_inc(weights_in, 16)
            sp.dma_start(bias0[:, :], b0.rearrange("(a f) -> a f", a=1).broadcast_to([P, F])).then_inc(weights_in, 16)
            sp.wait_ge(tails_set, 3)
            for t in range(2):
                sp.dma_start(wmsg_n[:, t, 0:2 * F + 1], wmsg[t]).then_inc(weights_in, 16)
                sp.dma_start(wmsg_n[:, t, 2 * F + 1:], bmsg[t].rearrange("(m o) -> m o", o=1)).then_inc(weights_in, 16)
                sp.dma_start(wih_n[:, t], wih[t].rearrange("(k p) m -> p k m", p=96)).then_inc(weights_in, 16)
                sp.dma_start(whh_n[:, t], whh[t].rearrange("(k p) m -> p k m", p=96)).then_inc(weights_in, 16)
                row = lambda a: a.rearrange("(o n) -> o n", o=1)
                sp.dma_start(wc2[F + 2:F + 3, t, 0:3 * F], row(bih[t])).then_inc(weights_in, 16)
                sp.dma_start(wc2[F + 3:F + 4, t, 0:2 * F], row(bhh[t, 0:2 * F])).then_inc(weights_in, 16)
                sp.dma_start(wc2[F + 3:F + 4, t, 3 * F:], row(bhh[t, 2 * F:])).then_inc(weights_in, 16)
            sp.wait_ge(keys_made, 2)
            sp.wait_ge(parts_made, 2)
            rec_rows = recs.rearrange("(r n) -> r n", n=EP * REC)
            sp.dma_start(rec_rows[0:112], rec[0:112]).then_inc(records_out, 16)
            sp.dma_start(rec_rows[112:], rec[112:P]).then_inc(records_out, 16)
            sp.wait_ge(records_out, 32)
            sp.wait_ge(starts_ready, 2)
            general = sp.value_load(flag_i[0:1, 0:1], min_val=0, max_val=1)
            with sp.If(general == 0):
                def load(i, ahead, first=False):
                    p, q = PAIRS * i + ahead, ahead % PAIRS
                    if not first:
                        sp.wait_ge(hots_ready, p - PAIRS + 1)
                    for w in range(2):
                        k = 2 * ahead + w
                        start = sp.value_load(starts[0:1, k:][:, bass.ds(2 * PAIRS * i, 1)])
                        sp.dma_start(record[:, q, w].rearrange("p j r -> p (j r)"),
                                     recs[bass.ds(start, WCAP * REC)].rearrange("(p n) -> p n", p=128)
                                     ).then_inc(record_in[q], 16)

                def store(i, q, n=2):
                    p, o = PAIRS * i + q, q - n + 1
                    sp.wait_ge(pair_out, 2 * (p + 1))
                    sp.dma_start(weight_sums[:, bass.ds((PAIRS * i + o) * 2 * KEYS, n * 2 * KEYS)],
                                 herows[P:128, o:o + n].rearrange("p q w k -> p (q w k)")).then_inc(wsum_out[q // 2], 16)

                AHEAD = PAIRS - 1
                for q in range(AHEAD):
                    load(0, q, first=True)
                for p in range(PAIRS):
                    load(0, p + AHEAD, first=p == 0)
                    if p == 3:
                        store(0, 1)
                with sp.Fori(1, TURNS - 1) as i:
                    for q in range(PAIRS):
                        load(i, q + AHEAD)
                        if q % 2:
                            store(i - (q == 1), (q - 2) % PAIRS)
                for p in range(PAIRS * (TURNS - 1), NPAIR):
                    if p + AHEAD < NPAIR:
                        load(p // PAIRS, p % PAIRS + AHEAD)
                    if p % 2:
                        store((p - 2) // PAIRS, (p - 2) % PAIRS)
                last = (NPAIR - 1) // 2 * 2
                for p in range(last - 2, NPAIR, 2):
                    n = min(2, NPAIR - p)
                    store(p // PAIRS, p % PAIRS + n - 1, n=n)
                for h in range(2):
                    sp.wait_ge(wsum_out[h], 16 * (TURNS + (NPAIR % PAIRS > 2 * h)))
                sp.wait_ge(counted, 1)
                for k in range(3):
                    sp.dma_start(wsums[:, k], weight_sums[k, 0:N * NB].rearrange("(b p c) -> p b c", p=P, c=NB)
                                 ).then_inc(wsum_in, 16)
            with sp.Else():
                for k in range(4):
                    if k > 0:
                        if k == 1:
                            sp.wait_ge(dve, at["features", False])
                        else:
                            sp.wait_ge(state_ready, (k - 1) * NG)
                        sp.dma_start(feat_rows.rearrange("(b p) f -> p b f", p=P), g_rows).then_inc(g_rows_out, 16)
                        sp.wait_ge(g_rows_out, 16 * k)
                    else:
                        sp.wait_ge(dve, at["ones"])
                    with sp.Fori(0, EP) as r:
                        sp.wait_ge(g_added, 4 * (k * EP + r))
                        chunk = lambda a: a[bass.ds(r * P, P)].rearrange("(p o) -> p o", o=1)
                        sp.dma_start(g_idx[:, 0:1], chunk(dst)).then_inc(g_in, 16)
                        sp.dma_start(g_idx[:, 1:2], chunk(src)).then_inc(g_in, 16)
                        sp.dma_start(g_wgt, ew[bass.ds(r * P, P), :]).then_inc(g_in, 16)
            for g in range(NG):
                sp.wait_ge(result_ready, g + 1)
                sp.dma_start(out_v[:, blocks(g), :], xs[:, blocks(g), :]).then_inc(stored, 16)
            sp.wait_ge(stored, 16 * NG)


_INS = ["x", "src", "dst", "edge_weight1", "L0_gnn_W", "L0_gnn_b", "L1_gnn_W_msg", "L1_gnn_b_msg",
        "L1_gnn_W_ih", "L1_gnn_W_hh", "L1_gnn_b_ih", "L1_gnn_b_hh"]


def kernel(**inputs):
    import concourse.bacc as bacc
    from concourse.bass_utils import run_bass_kernel_spmd

    nc = bacc.Bacc("TRN2", target_bir_lowering=False, num_devices=1, dynamic_dma_scratch_size=8192)
    arrays, args = {}, []
    for name in _INS:
        a = np.ascontiguousarray(inputs[name])
        arrays[f"in_{name}"] = a
        args.append(nc.dram_tensor(f"in_{name}", a.shape, mybir.dt.from_np(a.dtype), kind="ExternalInput").ap())
    out = nc.dram_tensor("out", (N, F), F32, kind="ExternalOutput").ap()
    build_program(nc, *args, out)
    return run_bass_kernel_spmd(nc, [arrays], core_ids=[0]).results[0]["out"]
```

```python
import numpy as np
import concourse.bass as bass
import concourse.mybir as mybir
from concourse.alu_op_type import AluOpType as ALU

F32, BF16, FP16, I32 = mybir.dt.float32, mybir.dt.bfloat16, mybir.dt.float16, mybir.dt.int32
U32 = mybir.dt.uint32
ACT = mybir.ActivationFunctionType
AX = mybir.AxisListType

N, F, E = 3125, 64, 103125
P, NB = 125, 25
EROWS, EP = 125, 825
D = 13
SLOTS = 4
WCAP = 128 * SLOTS
KEYS = D * NB
KPAD = KEYS + 1
NPAIR = -(-N // (2 * D))
PAIRS = 8
TURNS = NPAIR // PAIRS
NW = 2 * NPAIR
RING = 4
DC = NW * D
NWT = 256
COUNT_MAX = 256
MAGIC = 1.5 * 2 ** 23
EPS = 1e-5
GROUPS = [range(0, 4), range(4, 8), range(8, 12), range(12, 16), range(16, 20), range(20, 23), range(23, 25)]
G, NG = 4, len(GROUPS)
PARTS = 3 * F
SLOT = 256
XW = F + 4
GATES = 4 * F
REC = 4
ACC = F + 2
PH_WORDS = 9010


def build_program(nc, x, src, dst, ew, w0, b0, wmsg, bmsg, wih, whh, bih, bhh, out):
    from contextlib import ExitStack
    ctx = ExitStack()
    sb = lambda name, shape, dt: ctx.enter_context(nc.sbuf_tensor(name, shape, dt))
    sem = lambda name: ctx.enter_context(nc.semaphore(name))

    recs = nc.dram_tensor("edge_records", (E * REC,), F32).ap()
    weight_sums = nc.dram_tensor("weight_sums", (3, DC * NB), F32).ap()
    feat_rows = nc.dram_tensor("feature_rows", (N, F), F32).ap()

    with ctx:
        counts = sb("counts", [128, NB, DC], BF16)
        xs = sb("xs", [P, NB, F], F32)
        state = sb("state", [P, NB, XW], F32)
        ident = sb("ident", [128, 128], F32)
        identb = sb("identb", [128, 128], BF16)
        w01 = sb("w01", [128, F], F32)
        bias0 = sb("bias0", [P, F], F32)
        wc1 = sb("wc1", [128, 2, 3 * F], F32)
        wc2 = sb("wc2", [XW, 2, GATES], F32)
        dis = sb("dis", [P, NB], F32)
        ndis = sb("ndis", [P, NB], F32)
        small = sb("small", [128, 64], F32)
        starts = sb("starts", [1, NWT], I32)
        flag_i = sb("flag_i", [1, 1], I32)
        phase = sb("phase", [128, PH_WORDS], F32)
        ps = ctx.enter_context(nc.psum_tensor("ps", [128, 8, 512], F32))

        class Carve:
            def __init__(self, flat, size):
                self.flat, self.at, self.size = flat, 0, size
            def __call__(self, words, parts=128, dt=F32):
                v = self.flat[0:parts, self.at:self.at + words]
                self.at += words
                assert self.at <= self.size, (self.at, self.size)
                return v if dt == F32 else v.bitcast(dt)

        flat = counts[:, :, :].rearrange("p a b -> p (a b)").bitcast(F32)
        e = Carve(flat, NB * DC // 2)
        dstx = e(EP + COUNT_MAX, dt=I32)
        srci = e(EP, dt=I32)
        wgt = e(EP)
        rec = e(EP * REC)
        key_b, key_q, tmp_a, tmp_b = e(EP), e(EP), e(EP), e(EP)
        he_r = e(EP)
        rows_i = e(2 * EP, dt=I32).rearrange("p (g n) -> p g n", g=2)
        junk = e(2 * EP).rearrange("p (g n) -> p g n", g=2)
        wih_n = e(4 * 128, parts=96).rearrange("p (t g k) -> p t g k", t=2, g=2)
        whh_n = e(4 * F, parts=96).rearrange("p (t g k) -> p t g k", t=2, g=2)
        wmsg_n = e(2 * 130).rearrange("p (t k) -> p t k", t=2)
        wihT = e(2 * 3 * F).rearrange("p (t k) -> p t k", t=2)
        ln_b = e(NB * F, parts=P).rearrange("p (b f) -> p b f", f=F)
        rec3 = rec.rearrange("p (n r) -> p n r", r=REC)
        rec16 = rec.bitcast(BF16).rearrange("p (n r) -> p n r", r=2 * REC)

        g_ = Carve(flat, NB * DC // 2)
        iota_n = g_(N, parts=P)
        hot_n = g_(N, parts=P)
        acc = g_(NB * ACC, parts=P).rearrange("p (b f) -> p b f", f=ACC)
        g_idx = g_(2, parts=P, dt=I32)
        g_idf, g_wgt = g_(1, parts=P), g_(1, parts=P)
        g_msg = g_(ACC, parts=P)
        g_rows = g_(NB * F, parts=P).rearrange("p (b f) -> p b f", f=F)

        b_ = Carve(phase[:, :], PH_WORDS)
        iota_k = b_(2 * KPAD * SLOTS // 2, dt=FP16).rearrange("p (w k j) -> p w k j", w=2, j=SLOTS)
        iota_s = b_(128 * SLOTS // 2, dt=FP16).rearrange("p (k j) -> p k j", j=SLOTS)
        record = b_(PAIRS * 2 * SLOTS * REC).rearrange("p (q w j r) -> p q w j r", q=PAIRS, w=2, r=REC)
        record16 = record.rearrange("p q w j r -> p (q w j r)").bitcast(BF16).rearrange(
            "p (q w j r) -> p q w j r", q=PAIRS, w=2, r=2 * REC)
        key_row = b_(RING * 2 * SLOTS, dt=FP16).rearrange("p (q r m) -> p q r m", q=RING, r=2)
        hot_s = b_(2 * 2 * SLOTS * 64, dt=BF16).rearrange("p (h w k j) -> p h w k j", h=2, w=2, j=SLOTS)
        hot_k = b_(2 * 2 * SLOTS * KPAD // 2, dt=BF16).rearrange("p (h w k j) -> p h w k j", h=2, w=2, j=SLOTS)
        herows = b_(RING * 2 * KEYS).rearrange("p (q w k) -> p q w k", q=RING, w=2)
        pair_off = b_(2 * NPAIR).rearrange("p (r n) -> p r n", r=2)
        zeros = b_((KEYS + 1) // 2 + 1, dt=BF16)

        r_ = Carve(phase[:, :], PH_WORDS)
        parts = [r_((NB * (PARTS + 1) + 1) // 2, dt=BF16)[:, 0:NB * (PARTS + 1)].rearrange(
            "p (b f) -> p b f", f=PARTS + 1) for _ in range(2)]
        x1 = [r_(G * 2 * F, parts=P).rearrange("p (b f) -> p b f", f=2 * F) for _ in range(2)]
        x2 = [r_(G * XW, parts=P).rearrange("p (b f) -> p b f", f=XW) for _ in range(2)]
        scaled = parts[1].rearrange("p b f -> p (b f)")[0:P, 0:2 * NB * F].bitcast(F32).rearrange("p (b f) -> p b f", f=F)
        wsums = phase[0:P, r_.at:r_.at + 3 * NB * NB].rearrange("p (k b c) -> p k b c", k=3, b=NB)
        assert 3 * NB * NB <= 4 * 2 * P + G * 4 * F
        xT = r_(4 * 2 * P).rearrange("p (b c n) -> p b c n", b=4, c=2)
        rz = r_(G * 2 * F, parts=P).rearrange("p (b f) -> p b f", f=2 * F)
        nn = r_(G * 2 * F, parts=P).rearrange("p (b f) -> p b f", f=2 * F)
        ua = r_(G * F, parts=P).rearrange("p (b f) -> p b f", f=F)
        ub = r_(G * F, parts=P).rearrange("p (b f) -> p b f", f=F)
        stat = r_(4 * G, parts=P).rearrange("p (k b) -> p k b", k=4)

        thr, cnt, rowi, rp = small[:, 0:2], small[:, 2:4], small[:, 4:6], small[:, 6:8]
        rowi_i, rowi_u = small[:, 8:10].bitcast(I32), small[:, 8:10].bitcast(U32)
        viol, dst0, ones_c = small[0:P, 18:20], small[0:P, 11:12], small[:, 12:13]
        flag_f, span = small[0:1, 14:15], small[0:1, 15:16]
        cnt2 = small[:, 16:18]
        reach = e(NWT, parts=1)
        lns = sb("lns", [P, 4, NB], F32)

        ps_win = [ps[:, 2 * q:2 * q + 2, :] for q in range(2)]
        ps_deg, ps_misc = ps[:, 4, :], ps[:, 5, :]
        ps_wt = [ps[:, 6, :], ps[:, 7, :]]
        ps_sum = [ps[:, 2 * k:2 * k + 2, :].rearrange("p a (c f) -> p (a c) f", f=SLOT) for k in range(2)]
        ps_T = [ps[:, 4 + k, :].rearrange("p (s n) -> p s n", s=4) for k in range(2)]
        ps_G = [ps[:, 6 + k, 0:GATES] for k in range(2)]

        tails_set = sem("tails_set")
        dst_in, src_in, wgt_in, x_in = sem("dst_in"), sem("src_in"), sem("wgt_in"), sem("x_in")
        weights_in = sem("weights_in")
        ids_made, tables_made = sem("ids_made"), sem("tables_made")
        dve = sem("dve_done")
        pool = sem("pool_done")
        actc = sem("act_done")
        pec = sem("pe_done")
        rowidx_ready, rows_in = sem("rowidx_ready"), [sem("rows_in0"), sem("rows_in1")]
        keys_made = sem("keys_made")
        weights_rounded = sem("weights_rounded")
        viol_made = sem("viol_made")
        products_out = sem("products_out")
        centred, squared = sem("centred"), sem("squared")
        records_out = sem("records_out")
        starts_ready = sem("starts_ready")
        record_in = [sem(f"record_in{q}") for q in range(PAIRS)]
        keys_ready = sem("keys_ready")
        weights_ready = sem("weights_ready")
        hots_ready = sem("hots_ready")
        pair_summed = sem("pair_summed")
        pair_out = sem("pair_out")
        wsum_out = [sem(f"wsum_out{h}") for h in range(2)]
        wsum_in = sem("wsum_in")
        scaled_ready = sem("scaled_ready")
        features_ready = sem("features_ready")
        rounded = sem("rounded")
        counted = sem("counted")
        state_ready = sem("state_ready")
        sums_ready = sem("sums_ready")
        x1_state, x1_ready = sem("x1_state"), sem("x1_ready")
        trans_done = sem("trans_done")
        trans_out = sem("trans_out")
        gates_done = sem("gates_done")
        gates_out = sem("gates_out")
        tanh_in, tanh_out = sem("tanh_in"), sem("tanh_out")
        var_in, std_out = sem("var_in"), sem("std_out")
        result_ready, stored = sem("result_ready"), sem("stored")
        g_tables, g_rows_out, g_in, g_gathered = sem("g_tables"), sem("g_rows_out"), sem("g_in"), sem("g_gathered")
        g_weighed = sem("g_weighed")
        g_hot, g_summed, g_added = sem("g_hot"), sem("g_summed"), sem("g_added")

        def chain_of(eng, s):
            count = [0]
            def link(ins, wait=True):
                count[0] += 1
                ins.then_inc(s, 1)
                if wait:
                    eng.wait_ge(s, count[0])
                return count[0]
            link.count = count
            return link

        dst_rows = dst.rearrange("(r n) -> r n", n=EP)
        src_rows = src.rearrange("(r n) -> r n", n=EP)
        wgt_rows = ew.rearrange("(r n) o -> r (n o)", n=EP)
        out_v = out.rearrange("(b p) f -> p b f", p=P)
        N_WEIGHTS = 2 + 2 * 7

        def out_count(t, k):
            if isinstance(k, int) and k < 0:
                return out_count(t - 1, k + NB)
            return k + 1 if t == 0 else NB + 2 * NB * (t - 1) + 2 * (k + 1)

        def blocks(g):
            return slice(GROUPS[g][0], GROUPS[g][-1] + 1)

        def wsum_stores(h):
            return 16 * (NPAIR // RING + (NPAIR % RING > 2 * h))

        def products(g):
            return (nn, rz)[g % 2]

        chunks = [slice(0, 5), slice(5, 14), slice(14, NB)]
        SPLIT_ORDER = [(0, 0), (0, 1), (1, 0), (0, 2), (2, 0), (1, 1), (1, 2), (2, 1), (2, 2)]
        round_order = [s for s in SPLIT_ORDER if s[0] < 2]

        at = {}

        block = ctx.enter_context(nc.Block())

        @block.vector
        def _(v):
            link = chain_of(v, dve)
            tt, ts, stt = nc.vector.tensor_tensor, nc.vector.tensor_scalar, nc.vector.scalar_tensor_tensor
            red = nc.vector.tensor_reduce

            nc.vector.memset(dstx[96:128, EP:], 1 << 20).then_inc(tails_set, 1)
            nc.vector.memset(zeros, 0.0).then_inc(tails_set, 1)
            nc.vector.memset(wc2[:, :, :], 0.0).then_inc(tails_set, 1)
            nc.vector.memset(rec16[0:P, :, 7], 0.0).then_inc(tails_set, 1)
            nc.vector.memset(ones_c, 1.0).then_inc(tails_set, 1)
            link(nc.vector.memset(state[:, :, F + 2:], 1.0))

            v.wait_ge(dst_in, 48)
            link(nc.vector.tensor_copy(dst0, dstx[0:P, 0:1]))
            at["dst0"] = link.count[0]
            v.wait_ge(pec, 1)
            v.wait_ge(tables_made, 1)
            for g in range(2):
                link(ts(junk[:, g, 0:P], ps_misc[:, 0:P], thr[:, g:g + 1], 0.0, ALU.is_lt, ALU.add,
                        accum_out=cnt[:, g:g + 1]), wait=(g == 1))
            link(ts(rowi, cnt, -1.0, 0.0, ALU.add, ALU.max))
            nc.vector.tensor_copy(rowi_i, rowi).then_inc(rowidx_ready, 1)

            v.wait_ge(src_in, 16)
            link(ts(key_q[0:P], srci[0:P], 1.0 / P, -0.5 + 0.5 / P, ALU.mult, ALU.add))
            link(ts(key_b[0:P], key_q[0:P], MAGIC, -MAGIC, ALU.add, ALU.add))
            stt(rec3[0:P, :, 1], key_b[0:P], -float(P), srci[0:P], ALU.mult, ALU.add).then_inc(keys_made, 1)
            v.wait_ge(weights_rounded, 1)
            link(tt(he_r[0:P], wgt[0:P], rec16[0:P, :, 4], ALU.subtract))
            at["he_r"] = link.count[0]
            stt(rec3[0:P, :, 0], dstx[0:P, 0:EP], float(NB), key_b[0:P], ALU.mult, ALU.add).then_inc(keys_made, 1)
            v.wait_ge(weights_rounded, 2)
            tt(rec16[0:P, :, 6], he_r[0:P], rec16[0:P, :, 5], ALU.subtract).then_inc(keys_made, 1)

            v.wait_ge(x_in, 16)
            bc = lambda a, n=NB: a.unsqueeze(2).broadcast_to([P, n, F])
            link(red(lns[:, 0, :], xs[:, :, :], AX.X, ALU.add))
            link(ts(lns[:, 1, :], lns[:, 0, :], 1.0 / F, None, ALU.mult))
            at["mean0"] = link.count[0]

            for g in range(2):
                v.wait_ge(rows_in[g], 16)
                link(ts(junk[:, g, :], rows_i[:, g, :], thr[:, g:g + 1], 0.0, ALU.is_lt, ALU.add,
                        accum_out=cnt2[:, g:g + 1]), wait=(g == 1))
            link(stt(rp, rowi, float(EP), cnt2, ALU.mult, ALU.add))
            at["rp"] = link.count[0]
            stt(tmp_a[0:P], dstx[0:P, 1:EP + 1], 0.0, dstx[0:P, 0:EP], ALU.add, ALU.is_lt, accum_out=viol[:, 0:1]).then_inc(viol_made, 1)
            stt(tmp_b[0:P], dstx[0:P, COUNT_MAX:COUNT_MAX + EP], 0.0, dstx[0:P, 0:EP], ALU.add, ALU.is_equal,
                accum_out=viol[:, 1:2]).then_inc(viol_made, 1)
            v.wait_ge(pec, 5)
            first = ps_misc[0:1, 128:128 + NWT]
            ts(starts[0:1, :], first, float(E - WCAP), float(REC), ALU.min, ALU.mult).then_inc(starts_ready, 1)
            v.wait_ge(starts_ready, 1)
            link(stt(reach[0:1, 0:NWT - 1], first[:, 1:], float(REC), starts[0:1, 0:NWT - 1], ALU.mult, ALU.subtract))
            link(red(span, reach[0:1, 0:NWT - 1], AX.X, ALU.max))
            link(stt(flag_f, span, float(REC * WCAP), ps_misc[0:1, 400:401], ALU.is_gt, ALU.add))
            ts(flag_i[0:1, :], flag_f, 1.0, None, ALU.min).then_inc(starts_ready, 1)

            v.wait_ge(squared, 1)
            link(red(lns[:, 2, :], ln_b, AX.X, ALU.add))
            link(ts(lns[:, 2, :], lns[:, 2, :], 1.0 / F, EPS, ALU.mult, ALU.add))
            at["var0"] = link.count[0]

            def finish_first_norm(fast):
                v.wait_ge(actc, 1)
                link(nc.vector.reciprocal(lns[:, 0, :], lns[:, 3, :]))
                link(stt(state[:, :, 0:F], state[:, :, 0:F], 0.0, bc(lns[:, 0, :]), ALU.max, ALU.mult))
                at["state0", fast] = link.count[0]

            v.wait_ge(starts_ready, 2)
            general = v.value_load(flag_i[0:1, 0:1], min_val=0, max_val=1)

            def write_parts(to, gb, source, a):
                hi, mid, lo = (parts[to][0:P, gb, k * F:(k + 1) * F] for k in range(3))
                link(nc.vector.tensor_copy(hi, source))
                link(tt(a, source, hi, ALU.subtract))
                link(nc.vector.tensor_copy(mid, a))
                return tt(lo, a, mid, ALU.subtract)

            def scale_by_degree(fast):
                link(ts(lns[:, 1, :], lns[:, 0, :], 1.0, None, ALU.max), wait=False)
                link(ts(lns[:, 2, :], lns[:, 0, :], 1.0, None, ALU.min))
                at["degree", fast] = link.count[0]
                if fast:
                    link(nc.vector.memset(parts[0][0:P, :, PARTS:], 1.0))
                v.wait_ge(actc, 2)
                link(nc.vector.reciprocal(dis[:, :], lns[:, 3, :]))
                link(tt(dis[:, :], dis[:, :], lns[:, 2, :], ALU.mult))
                if not fast:
                    link(ts(ndis[:, :], dis[:, :], -1.0, None, ALU.mult))
                    link(tt(g_rows, state[:, :, 0:F], bc(dis[:, :]), ALU.mult))
                    at["scaled"] = link.count[0]
                    return
                for k, c in SPLIT_ORDER:
                    gb = chunks[c]
                    if k > 0:
                        v.wait_ge(rounded, round_order.index((k - 1, c)) + 1)
                        taken = parts[0][0:P, gb, (k - 1) * F:k * F]
                    if k == 0:
                        tt(scaled[:, gb], state[:, gb, 0:F], bc(dis[:, gb], gb.stop - gb.start), ALU.mult).then_inc(scaled_ready, 1)
                    elif k == 1:
                        tt(scaled[:, gb], scaled[:, gb], taken, ALU.subtract).then_inc(scaled_ready, 1)
                    else:
                        tt(parts[0][0:P, gb, 2 * F:PARTS], scaled[:, gb], taken, ALU.subtract).then_inc(features_ready, 1)
                link(ts(ndis[:, :], dis[:, :], -1.0, None, ALU.mult))

            def gathered_sums(k, index, width):
                link(nc.vector.memset(acc[:, :, :], 0.0))
                with v.Fori(0, EP) as r:
                    v.wait_ge(g_in, 48 * (k * EP + r + 1))
                    nc.vector.tensor_copy(g_idf, g_idx[:, index:index + 1]).then_inc(g_hot, 1)
                    v.wait_ge(g_hot, 2 * (k * EP + r) + 1)
                    ts(hot_n, iota_n, g_idf, None, ALU.is_equal).then_inc(g_hot, 1)
                    v.wait_ge(g_summed, k * EP + r + 1)
                    for b in range(4):
                        n = min(7, NB - 7 * b)
                        a = acc[:, 7 * b:7 * b + n, 0:width]
                        s = ps[0:P, b, 0:7 * ACC].rearrange("p (s f) -> p s f", f=ACC)[:, 0:n, 0:width]
                        tt(a, a, s, ALU.add).then_inc(g_added, 1)
                    v.wait_ge(g_added, 4 * (k * EP + r + 1))

            def sums_to_x1(t, g, fast):
                gb, n, K = blocks(g), len(GROUPS[g]), t * NG + g
                x = x1[K % 2][:, 0:n, F:]
                v.wait_ge(x1_state, K + 1)
                if fast:
                    v.wait_ge(sums_ready, K + 1)
                    s = ps_sum[K % 2]
                    u = ua[:, 0:n]
                    i = red(u if t == 0 else x, s[0:P, 0:n, 0:PARTS].rearrange("p b (k f) -> p b f k", k=3),
                            AX.X, ALU.add)
                    if t > 0:
                        i.then_inc(x1_ready, 1)
                        return
                    link(i, wait=False)
                    link(nc.vector.tensor_copy(state[:, gb, F + 1:F + 2], s[0:P, 0:n, PARTS:PARTS + 1]))
                    tt(x, u, bc(ndis[:, gb], n), ALU.mult).then_inc(x1_ready, 1)
                elif t > 0:
                    nc.vector.tensor_copy(x, acc[:, gb, 0:F]).then_inc(x1_ready, 1)
                else:
                    link(nc.vector.tensor_copy(state[:, gb, F + 1:F + 2], acc[:, gb, F:F + 1]))
                    link(nc.vector.tensor_copy(state[:, gb, F:F + 1], acc[:, gb, F + 1:F + 2]))
                    tt(x, acc[:, gb, 0:F], bc(ndis[:, gb], n), ALU.mult).then_inc(x1_ready, 1)

            def finish_first(g):
                gb, n = blocks(g), len(GROUPS[g])
                v.wait_ge(gates_out, out_count(0, GROUPS[g][-1]))
                bias = bias0[:, :].unsqueeze(1).broadcast_to([P, n, F])
                a, b, st = ua[:, 0:n], ub[:, 0:n], stat[:, :, 0:n]
                link(tt(a, products(g)[:, 0:n, 0:F], bias, ALU.add))
                link(stt(xs[:, gb, :], a, 0.0, xs[:, gb, :], ALU.max, ALU.add))
                link(red(st[:, 0, :], xs[:, gb, :], AX.X, ALU.add))
                link(stt(a, bc(st[:, 0, :], n), -1.0 / F, xs[:, gb, :], ALU.mult, ALU.add))
                link(tt(b, a, a, ALU.mult))
                link(red(st[:, 2, :], b, AX.X, ALU.add))
                ts(st[:, 2, :], st[:, 2, :], 1.0 / F, EPS, ALU.mult, ALU.add).then_inc(var_in, 1)
                v.wait_ge(std_out, g + 1)
                link(nc.vector.reciprocal(st[:, 0, :], st[:, 3, :]))
                return stt(state[:, gb, 0:F], a, 0.0, bc(st[:, 0, :], n), ALU.max, ALU.mult)

            def finish_gru(t, g):
                gb, n = blocks(g), len(GROUPS[g])
                v.wait_ge(gates_out, out_count(t, GROUPS[g][-1]))
                a, b = ua[:, 0:n], ub[:, 0:n]
                link(tt(a, rz[:, 0:n, 0:F], nn[:, 0:n, F:], ALU.mult))
                tt(a, a, nn[:, 0:n, 0:F], ALU.add).then_inc(tanh_in, 1)
                v.wait_ge(tanh_out, (t - 1) * NG + g + 1)
                link(tt(a, state[:, gb, 0:F], b, ALU.subtract))
                link(tt(a, a, rz[:, 0:n, F:], ALU.mult))
                return tt(state[:, gb, 0:F], a, b, ALU.add)

            def rounds(t, fast):
                if t == 0 and fast:
                    v.wait_ge(wsum_in, 48)
                    link(red(state[:, :, F:F + 1], wsums.rearrange("p k b c -> p b k c"), AX.XY, ALU.add))
                for g in range(NG + 1):
                    if g < NG:
                        sums_to_x1(t, g, fast)
                    if g == 0:
                        continue
                    gb = blocks(g - 1)
                    i = finish_first(g - 1) if t == 0 else finish_gru(t, g - 1)
                    if t == 2:
                        link(i)
                        tt(xs[:, gb, :], state[:, gb, 0:F], xs[:, gb, :], ALU.add).then_inc(result_ready, 1)
                    elif fast:
                        link(i)
                        i = write_parts((t + 1) % 2, gb, state[:, gb, 0:F], ua[:, 0:len(GROUPS[g - 1])])
                    else:
                        link(i)
                        i = nc.vector.tensor_copy(g_rows[:, gb, :], state[:, gb, 0:F])
                    if t < 2:
                        i.then_inc(state_ready, 1)
                        v.wait_ge(state_ready, t * NG + g)

            base = link.count[0]

            with v.If(general == 0):
                def one_hots(p, q, first=False):
                    h = q % 2
                    v.wait_ge(keys_ready, p + 1)
                    if not first:
                        v.wait_ge(pair_summed, p - 1)
                    of = lambda r, n: key_row[:, q % RING, r, :].rearrange("p (w j) -> p w j", w=2).unsqueeze(
                        2).broadcast_to([128, 2, n, SLOTS])
                    tt(hot_s[:, h, :, 0:P, :], iota_s[:, 0:P, :].unsqueeze(1).broadcast_to([128, 2, P, SLOTS]),
                       of(1, P), ALU.is_equal)
                    tt(hot_k[:, h, :, 0:KEYS, :], iota_k[:, :, 0:KEYS, :], of(0, KEYS), ALU.is_equal).then_inc(hots_ready, 1)

                v.wait_ge(tables_made, 5)
                for q in range(PAIRS):
                    one_hots(q, q, first=q < 2)
                with v.Fori(1, TURNS) as i:
                    for q in range(PAIRS):
                        one_hots(PAIRS * i + q, q)
                for p in range(PAIRS * TURNS, NPAIR):
                    one_hots(p, p % PAIRS)
                finish_first_norm(True)
                v.wait_ge(counted, 1)
                link(red(lns[:, 0, :], ps_deg[0:P, 0:KEYS].rearrange("p (b d) -> p b d", d=D), AX.X, ALU.add))
                scale_by_degree(True)
                for t in range(3):
                    rounds(t, True)
            link.count[0] = base
            with v.Else():
                finish_first_norm(False)
                v.wait_ge(records_out, 32)
                link(nc.vector.memset(g_msg, 1.0))
                at["ones"] = link.count[0]
                v.wait_ge(g_tables, 1)
                gathered_sums(0, 1, 1)
                link(nc.vector.tensor_copy(lns[:, 0, :].unsqueeze(2), acc[:, :, 0:1]))
                scale_by_degree(False)
                for t in range(3):
                    gathered_sums(t + 1, 0, ACC)
                    rounds(t, False)

        @block.gpsimd
        def _(g):
            link = chain_of(g, pool)
            gp = nc.gpsimd
            link(gp.memset(ident[:, :], 0.0))
            link(gp.affine_select(out=ident[:, :], in_=ident[:, :], compare_op=ALU.not_equal, fill=1.0, base=0,
                                  pattern=[[-1, 128]], channel_multiplier=1))
            gp.tensor_copy(identb[:, :], ident[:, :]).then_inc(ids_made, 1)
            gp.iota(thr, [[128 * D, 2]], base=0, channel_multiplier=D, allow_small_or_imprecise_dtypes=True).then_inc(tables_made, 1)
            gp.iota(iota_s, [[1, 128], [0, SLOTS]], base=0, channel_multiplier=0, allow_small_or_imprecise_dtypes=True).then_inc(tables_made, 1)
            gp.memset(pair_off[:, 1, :], 0.0)
            gp.iota(pair_off[:, 0, :], [[2 * KEYS, NPAIR]], base=0, channel_multiplier=0,
                    allow_small_or_imprecise_dtypes=True).then_inc(tables_made, 1)
            g.wait_ge(rowidx_ready, 1)
            for k in range(2):
                gp.indirect_dma_start(rows_i[:, k, :], None, dst_rows,
                                      bass.IndirectOffsetOnAxis(ap=rowi_u[:, k:k + 1], axis=0)).then_inc(rows_in[k], 16)

            for w in range(2):
                gp.iota(iota_k[:, w, 0:KEYS, :].rearrange("p (b d) j -> p b d j", b=NB), [[1, NB], [NB, D], [0, SLOTS]],
                        base=w * KEYS, channel_multiplier=0,
                        allow_small_or_imprecise_dtypes=True).then_inc(tables_made, 1)
            g.wait_ge(dve, at["mean0"])
            gp.tensor_tensor(state[:, :, 0:F], xs[:, :, :], lns[:, 1, :].unsqueeze(2).broadcast_to([P, NB, F]),
                             ALU.subtract).then_inc(centred, 1)

            g.wait_ge(starts_ready, 2)
            general = g.value_load(flag_i[0:1, 0:1], min_val=0, max_val=1)

            def x1_state_half(t, n):
                gb, size, K = blocks(n), len(GROUPS[n]), t * NG + n
                if t > 0:
                    g.wait_ge(state_ready, (t - 1) * NG + n + 1)
                if K >= 2:
                    g.wait_ge(trans_done, NB * ((K - 2) // NG) + GROUPS[(K - 2) % NG][-1] + 1)
                if t == 0:
                    gp.tensor_copy(x1[K % 2][:, 0:size, 0:F], state[:, gb, 0:F]).then_inc(x1_state, 1)
                else:
                    link(gp.tensor_copy(x2[K % 2][:, 0:size], state[:, gb, :]))
                    gp.tensor_tensor(x1[K % 2][:, 0:size, 0:F], state[:, gb, 0:F],
                                     state[:, gb, F + 1:F + 2].broadcast_to([P, size, F]), ALU.mult).then_inc(x1_state, 1)

            base = link.count[0]
            with g.If(general == 0):
                def keys(i, ahead):
                    p, q = PAIRS * i + ahead, ahead % PAIRS
                    g.wait_ge(tables_made, 5)
                    g.wait_ge(record_in[q], 32 * (i + 1 + ahead // PAIRS))
                    if not (isinstance(p, int) and p < RING):
                        g.wait_ge(hots_ready, p - RING + 1)
                    if not (isinstance(p, int) and p < 3):
                        g.wait_ge(pair_summed, p - 2)
                    gp.tensor_tensor(key_row[:, q % RING], record[:, q, :, :, 0:2].rearrange("p w j r -> p r (w j)"),
                                     pair_off[:, :, bass.ds(p, 1)].broadcast_to([128, 2, 2 * SLOTS]),
                                     ALU.subtract).then_inc(keys_ready, 1)

                def weights(q):
                    gp.tensor_copy(hot_s[:, q % 2, :, P:, :],
                                   record16[:, q, :, :, 4:7].rearrange("p w j c -> p w c j")).then_inc(weights_ready, 1)

                keys(0, 0)
                for q in range(PAIRS):
                    keys(0, q + 1)
                    weights(q)
                with g.Fori(1, TURNS) as i:
                    for q in range(PAIRS):
                        keys(i, q + 1)
                        weights(q)
                for p in range(PAIRS * TURNS, NPAIR):
                    if p + 1 < NPAIR:
                        keys(p // PAIRS, p % PAIRS + 1)
                    else:
                        g.wait_ge(pair_summed, p - 1)
                    weights(p % PAIRS)
                g.wait_ge(counted, 1)
                for h in range(2):
                    g.wait_ge(wsum_out[h], wsum_stores(h))
                g.wait_ge(dve, at["state0", True])
                for t in range(3):
                    for n in range(NG):
                        x1_state_half(t, n)
            link.count[0] = base
            with g.Else():
                g.wait_ge(dve, at["ones"])
                gp.iota(iota_n, [[1, N]], base=0, channel_multiplier=0,
                        allow_small_or_imprecise_dtypes=True).then_inc(g_tables, 1)
                for t in range(3):
                    with g.Fori(0, EP) as r:
                        g.wait_ge(g_in, 48 * ((t + 1) * EP + r + 1))
                        gp.tensor_tensor(g_msg[:, F + 1:], g_wgt, g_msg[:, F:F + 1], ALU.mult).then_inc(g_weighed, 1)
                        g.wait_ge(g_rows_out, 16 * (t + 1))
                        gp.indirect_dma_start(g_msg[:, 0:F], None, feat_rows,
                                              bass.IndirectOffsetOnAxis(ap=g_idx[:, 1:2].bitcast(U32), axis=0)
                                              ).then_inc(g_gathered, 16)
                        g.wait_ge(g_gathered, 16 * (t * EP + r + 1))
                    for n in range(NG):
                        x1_state_half(t, n)

        @block.scalar
        def _(a):
            act = nc.scalar.activation
            a.wait_ge(wgt_in, 16)
            act(rec16[0:P, :, 4], wgt[0:P], ACT.Copy).then_inc(weights_rounded, 1)
            a.wait_ge(dve, at["he_r"])
            act(rec16[0:P, :, 5], he_r[0:P], ACT.Copy).then_inc(weights_rounded, 1)
            for t in range(2):
                a.wait_ge(pec, 2 + t)
                act(wihT[:, t, :], ps_wt[t][:, 0:3 * F], ACT.Copy).then_inc(products_out, 1)
                act(wc2[0:F, t, 0:2 * F], ps_wt[t][0:F, 192:320], ACT.Copy).then_inc(products_out, 1)
                act(wc2[0:F, t, 3 * F:], ps_wt[t][0:F, 320:384], ACT.Copy).then_inc(products_out, 1)
            for t in range(2):
                a.wait_ge(pec, 6 + t)
                act(wc1[:, t, :], ps_wt[t][:, 0:3 * F], ACT.Copy).then_inc(products_out, 1)
                act(wc2[F:F + 2, t, 0:3 * F], ps_wt[t][F:F + 2, 192:384], ACT.Copy).then_inc(products_out, 1)
            a.wait_ge(centred, 1)
            act(ln_b, state[:, :, 0:F], ACT.Square).then_inc(squared, 1)
            a.wait_ge(dve, at["var0"])
            act(lns[:, 3, :], lns[:, 2, :], ACT.Sqrt).then_inc(actc, 1)
            a.wait_ge(starts_ready, 2)
            general = a.value_load(flag_i[0:1, 0:1], min_val=0, max_val=1)

            def transposes_out(t, k):
                K = t * NB + k
                a.wait_ge(trans_done, K + 1)
                if K >= 4:
                    a.wait_ge(gates_done, K - 3)
                nc.scalar.copy(xT[:, K % 4, 0, :], ps_T[K % 2][:, 0, 0:P]).then_inc(trans_out, 1)
                if t > 0:
                    nc.scalar.copy(xT[0:XW, K % 4, 1, :], ps_T[K % 2][0:XW, 1, 0:P]).then_inc(trans_out, 1)

            def gates_to_sbuf(t, g, k):
                n, K = k - GROUPS[g][0], t * NB + k
                a.wait_ge(gates_done, K + 1)
                if n == 0 and t * NG + g > 0:
                    if t == 0:
                        if g >= 2:
                            a.wait_ge(state_ready, g - 1)
                    elif t < 2 or g == 0:
                        a.wait_ge(state_ready, t * NG + g)
                    else:
                        a.wait_ge(result_ready, g)
                if t == 0:
                    nc.scalar.copy(products(g)[:, n, 0:F], ps_G[K % 2][0:P, 0:F]).then_inc(gates_out, 1)
                else:
                    act(rz[:, n, :], ps_G[K % 2][0:P, 0:2 * F], ACT.Sigmoid).then_inc(gates_out, 1)
                    nc.scalar.copy(nn[:, n, :], ps_G[K % 2][0:P, 2 * F:]).then_inc(gates_out, 1)

            def group_function(t, g):
                n = len(GROUPS[g])
                if t == 0:
                    a.wait_ge(var_in, g + 1)
                    act(stat[:, 3, 0:n], stat[:, 2, 0:n], ACT.Sqrt).then_inc(std_out, 1)
                else:
                    a.wait_ge(tanh_in, (t - 1) * NG + g + 1)
                    act(ub[:, 0:n], ua[:, 0:n], ACT.Tanh).then_inc(tanh_out, 1)

            def rounds(fast):
                a.wait_ge(dve, at["degree", fast])
                act(lns[:, 3, :], lns[:, 1, :], ACT.Sqrt).then_inc(actc, 1)
                if fast:
                    for n, (k, c) in enumerate(round_order):
                        a.wait_ge(scaled_ready, n + 1)
                        act(parts[0][0:P, chunks[c], k * F:(k + 1) * F], scaled[:, chunks[c]], ACT.Copy).then_inc(rounded, 1)
                for t in range(3):
                    for g in range(NG):
                        for n, k in enumerate(GROUPS[g]):
                            transposes_out(t, k)
                            if t == 0 and g > 0 and n == 1:
                                group_function(t, g - 1)
                            if k > 0:
                                gates_to_sbuf(t, g - (n == 0), k - 1)
                            if t > 0 and g > 0 and n == 0:
                                group_function(t, g - 1)
                    gates_to_sbuf(t, NG - 1, NB - 1)
                    group_function(t, NG - 1)

            with a.If(general == 0):
                def evacuate(i, q, turn0=False):
                    p, h, r = PAIRS * i + q, q % 2, q % RING
                    if q % 2 == 0 and not (turn0 and q == 0):
                        store(p - 2, (q - 2) % RING)
                    a.wait_ge(pair_summed, p + 1)
                    act(counts[:, :, bass.ds(p * 2 * D, 2 * D)].rearrange("p b (w d) -> p w b d", w=2),
                        ps_win[h][:, :, 0:KEYS].rearrange("p w (b d) -> p w b d", d=D), ACT.Copy).then_inc(pair_out, 1)
                    if not (turn0 and q < RING):
                        a.wait_ge(wsum_out[r // 2], 16 * (PAIRS // RING * i + q // RING))
                    act(herows[96:128, r].rearrange("p w (d b) -> p w b d", d=D),
                        ps_win[h][96:128, :, 0:KEYS].rearrange("p w (b d) -> p w b d", d=D), ACT.Copy).then_inc(pair_out, 1)

                def store(p, r, n=2):
                    a.wait_ge(pair_out, 2 * (p + n))
                    a.dma_start(weight_sums[:, bass.ds(p * 2 * KEYS, n * 2 * KEYS)],
                                herows[P:128, r:r + n].rearrange("p q w k -> p (q w k)")).then_inc(wsum_out[r // 2], 16)

                for q in range(PAIRS):
                    evacuate(0, q, turn0=True)
                with a.Fori(1, TURNS) as i:
                    for q in range(PAIRS):
                        evacuate(i, q)
                for p in range(PAIRS * TURNS, NPAIR):
                    evacuate(p // PAIRS, p % PAIRS)
                last = (NPAIR - 1) // 2 * 2
                store(last, last % RING, n=NPAIR - last)
                rounds(True)
            with a.Else():
                rounds(False)

        @block.tensor
        def _(pe):
            mm = nc.tensor.matmul
            pe.wait_ge(ids_made, 1)
            pe.wait_ge(dve, at["dst0"])
            mm(ps_misc[:, 0:P], dst0.broadcast_to([P, 128]), ident[0:P, 0:P], start=True, stop=True).then_inc(pec, 1)
            pe.wait_ge(weights_in, 16 * N_WEIGHTS)
            for t in range(2):
                for k in range(2):
                    nc.tensor.transpose(ps_wt[t][:, 96 * k:96 * (k + 1)], wih_n[:, t, k, :], ident[0:96, 0:96])
                    last = nc.tensor.transpose(ps_wt[t][0:F, 192 + 96 * k:192 + 96 * (k + 1)], whh_n[:, t, k, :],
                                               ident[0:96, 0:96])
                last.then_inc(pec, 1)
            pe.wait_ge(dve, at["rp"])
            for k in range(2):
                last = mm(ps_misc[0:1, 128 * (k + 1):128 * (k + 2)], rp[:, k:k + 1], ident[:, :], start=True, stop=True)
            last.then_inc(pec, 1)
            pe.wait_ge(tails_set, 5)
            pe.wait_ge(viol_made, 2)
            for k in range(2):
                last = mm(ps_misc[0:1, 400:401], viol[:, k:k + 1], ones_c[0:P], start=(k == 0), stop=(k == 1))
            last.then_inc(pec, 1)
            for t in range(2):
                pe.wait_ge(products_out, 3 * (t + 1))
                mm(ps_wt[t][:, 0:3 * F], wmsg_n[:, t, 0:2 * F], wihT[:, t, :], start=True, stop=True)
                mm(ps_wt[t][F:F + 2, 192:384], wmsg_n[:, t, 2 * F:], wihT[:, t, :], start=True, stop=True).then_inc(pec, 1)
            pe.wait_ge(starts_ready, 2)
            general = pe.value_load(flag_i[0:1, 0:1], min_val=0, max_val=1)

            def after_block(s, t, k):
                if not (t == 0 and k < 0):
                    pe.wait_ge(s, out_count(t, k))

            def transpose_block(t, k):
                g = [k in blocks_of for blocks_of in GROUPS].index(True)
                n, K = k - GROUPS[g][0], t * NG + g
                if n == 0:
                    pe.wait_ge(x1_ready, K + 1)
                after_block(trans_out, t, k - 2)
                into = ps_T[(t * NB + k) % 2]
                i = nc.tensor.transpose(into[:, 0, 0:P], x1[K % 2][:, n, :], ident[0:P, 0:P])
                if t > 0:
                    i = nc.tensor.transpose(into[0:XW, 1, 0:P], x2[K % 2][:, n, :], ident[0:P, 0:P])
                i.then_inc(trans_done, 1)

            def gates_block(t, k):
                pe.wait_ge(trans_out, out_count(t, k))
                after_block(gates_out, t, k - 2)
                K = t * NB + k
                o, x = ps_G[K % 2][0:P, :], xT[:, K % 4]
                if t == 0:
                    mm(o[:, 0:F], x[:, 0, :], w01[:, :], start=True, stop=True).then_inc(gates_done, 1)
                else:
                    mm(o, x[0:XW, 1, :], wc2[:, t - 1, :], start=True, stop=False, skip_group_check=True)
                    mm(o[:, 0:3 * F], x[:, 0, :], wc1[:, t - 1, :], start=False, stop=True,
                       skip_group_check=True).then_inc(gates_done, 1)

            def step(t, k):
                transpose_block(t, k)
                if k > 0:
                    gates_block(t, k - 1)

            def sums(t, g, k, sources):
                n, width = k - GROUPS[g][0], PARTS + 1 if t == 0 else PARTS
                for s in sources:
                    last = mm(ps_sum[(t * NG + g) % 2][:, n, 0:width], counts[0:P, s, k * P:k * P + 128],
                              parts[t % 2][0:P, s, 0:width], start=(s == 0 and n % 2 == 0), stop=(s == NB - 1),
                              skip_group_check=True)
                if k == GROUPS[g][-1] and sources[-1] == NB - 1:
                    last.then_inc(sums_ready, 1)

            def first_group(t):
                if t == 0:
                    for c, gb in enumerate(chunks):
                        pe.wait_ge(features_ready, c + 1)
                        for k in GROUPS[0]:
                            sums(0, 0, k, range(gb.start, gb.stop))
                    return
                pe.wait_ge(x1_ready, t * NG - 1)
                late = range(NG - 3, NG)
                pe.wait_ge(state_ready, t * NG - len(late))
                tail = GROUPS[NG - 1]
                for n, k in enumerate(GROUPS[0]):
                    sums(t, 0, k, range(0, GROUPS[late[0]][0]))
                    if n < len(tail):
                        step(t - 1, tail[n])
                    if n == len(tail):
                        gates_block(t - 1, NB - 1)
                for g in late:
                    pe.wait_ge(state_ready, (t - 1) * NG + g + 1)
                    for k in GROUPS[0]:
                        sums(t, 0, k, GROUPS[g])

            def other_group(t, g):
                if t * NG + g >= 2:
                    pe.wait_ge(x1_ready, t * NG + g - 1)
                before = GROUPS[g - 1]
                for n, k in enumerate(GROUPS[g]):
                    sums(t, g, k, range(NB))
                    if n < len(before):
                        step(t, before[n])
                for k in before[len(GROUPS[g]):]:
                    step(t, k)

            with pe.If(general == 0):
                pe.wait_ge(tails_set, 5)
                mm(ps_deg[:, 0:KEYS], identb[:, :], zeros[:, 0:KEYS], start=True, stop=False, skip_group_check=True)

                def degrees(p):
                    pe.wait_ge(pair_out, 2 * p + 1)
                    for w in range(2):
                        mm(ps_deg[:, 0:KEYS].rearrange("p (b d) -> p b d", d=D), identb[:, :],
                           counts[:, :, bass.ds((2 * p + w) * D, D)], start=False, stop=False, skip_group_check=True)

                def pair(p, q, first=False):
                    h = q % 2
                    pe.wait_ge(hots_ready, p + 1)
                    pe.wait_ge(weights_ready, p + 1)
                    if not first:
                        pe.wait_ge(pair_out, 2 * (p - 1))
                    for m in range(2 * SLOTS):
                        w, j = m // SLOTS, m % SLOTS
                        last = mm(ps_win[h][:, w, 0:KEYS], hot_s[:, h, w, :, j], hot_k[:, h, w, 0:KEYS, j],
                                  start=(j == 0), stop=(j == SLOTS - 1))
                    last.then_inc(pair_summed, 1)

                for p in range(PAIRS):
                    pair(p, p, first=p < 2)
                    if p >= 2:
                        degrees(p - 2)
                with pe.Fori(1, TURNS) as i:
                    for q in range(PAIRS):
                        pair(PAIRS * i + q, q)
                        degrees(PAIRS * i + q - 2)
                for p in range(PAIRS * TURNS, NPAIR):
                    pair(p, p % PAIRS)
                    degrees(p - 2)
                degrees(NPAIR - 2)
                degrees(NPAIR - 1)
                mm(ps_deg[:, 0:KEYS], identb[:, :], zeros[:, 0:KEYS], start=False, stop=True,
                   skip_group_check=True).then_inc(counted, 1)
                for t in range(3):
                    first_group(t)
                    for g in range(1, NG):
                        other_group(t, g)
                for k in GROUPS[NG - 1]:
                    step(2, k)
                gates_block(2, NB - 1)
            with pe.Else():
                def gathered_sums(k, width):
                    with pe.Fori(0, EP) as r:
                        pe.wait_ge(g_hot, 2 * (k * EP + r + 1))
                        pe.wait_ge(g_in, 48 * (k * EP + r + 1))
                        if k > 0:
                            pe.wait_ge(g_weighed, (k - 1) * EP + r + 1)
                            pe.wait_ge(g_gathered, 16 * ((k - 1) * EP + r + 1))
                        for b in range(NB):
                            last = mm(ps[0:P, b // 7, ACC * (b % 7):ACC * (b % 7) + width], hot_n[:, b * P:(b + 1) * P],
                                      g_msg[:, 0:width], start=True, stop=True)
                        last.then_inc(g_summed, 1)
                gathered_sums(0, 1)
                for t in range(3):
                    gathered_sums(t + 1, ACC)
                    for k in range(NB):
                        step(t, k)
                    gates_block(t, NB - 1)

        @block.sync
        def _(sp):
            sp.wait_ge(tails_set, 1)
            def over(lo, hi):
                return bass.AP(dst.tensor, lo * EP, [[EP, hi - lo], [1, EP + COUNT_MAX]])
            sp.dma_start(dstx[0:112], over(0, 112)).then_inc(dst_in, 16)
            sp.dma_start(dstx[112:EROWS - 1], over(112, EROWS - 1)).then_inc(dst_in, 16)
            sp.dma_start(dstx[EROWS - 1:EROWS, 0:EP], dst_rows[EROWS - 1:EROWS, :]).then_inc(dst_in, 16)
            sp.dma_start(wgt[0:P], wgt_rows).then_inc(wgt_in, 16)
            sp.dma_start(srci[0:P], src_rows).then_inc(src_in, 16)
            sp.dma_start(xs[:, :, :], x.rearrange("(b p) f -> p b f", p=P)).then_inc(x_in, 16)
            sp.dma_start(w01[:, :], w0.rearrange("k i o -> (k i) o")).then_inc(weights_in, 16)
            sp.dma_start(bias0[:, :], b0.rearrange("(a f) -> a f", a=1).broadcast_to([P, F])).then_inc(weights_in, 16)
            sp.wait_ge(tails_set, 3)
            for t in range(2):
                sp.dma_start(wmsg_n[:, t, 0:2 * F + 1], wmsg[t]).then_inc(weights_in, 16)
                sp.dma_start(wmsg_n[:, t, 2 * F + 1:], bmsg[t].rearrange("(m o) -> m o", o=1)).then_inc(weights_in, 16)
                sp.dma_start(wih_n[:, t], wih[t].rearrange("(k p) m -> p k m", p=96)).then_inc(weights_in, 16)
                sp.dma_start(whh_n[:, t], whh[t].rearrange("(k p) m -> p k m", p=96)).then_inc(weights_in, 16)
                row = lambda a: a.rearrange("(o n) -> o n", o=1)
                sp.dma_start(wc2[F + 2:F + 3, t, 0:3 * F], row(bih[t])).then_inc(weights_in, 16)
                sp.dma_start(wc2[F + 3:F + 4, t, 0:2 * F], row(bhh[t, 0:2 * F])).then_inc(weights_in, 16)
                sp.dma_start(wc2[F + 3:F + 4, t, 3 * F:], row(bhh[t, 2 * F:])).then_inc(weights_in, 16)
            sp.wait_ge(tails_set, 4)
            sp.wait_ge(keys_made, 3)
            sp.wait_ge(weights_rounded, 2)
            rec_rows = recs.rearrange("(r n) -> r n", n=EP * REC)
            sp.dma_start(rec_rows[0:112], rec[0:112]).then_inc(records_out, 16)
            sp.dma_start(rec_rows[112:], rec[112:P]).then_inc(records_out, 16)
            sp.wait_ge(records_out, 32)
            sp.wait_ge(starts_ready, 2)
            general = sp.value_load(flag_i[0:1, 0:1], min_val=0, max_val=1)
            with sp.If(general == 0):
                def load(i, ahead, first=False):
                    p, q = PAIRS * i + ahead, ahead % PAIRS
                    if not first:
                        sp.wait_ge(weights_ready, p - PAIRS + 1)
                    for w in range(2):
                        k = 2 * ahead + w
                        start = sp.value_load(starts[0:1, k:][:, bass.ds(2 * PAIRS * i, 1)])
                        sp.dma_start(record[:, q, w].rearrange("p j r -> p (j r)"),
                                     recs[bass.ds(start, WCAP * REC)].rearrange("(p n) -> p n", p=128)
                                     ).then_inc(record_in[q], 16)

                AHEAD = PAIRS - 1
                for q in range(AHEAD):
                    load(0, q, first=True)
                for p in range(PAIRS):
                    load(0, p + AHEAD, first=p == 0)
                with sp.Fori(1, TURNS - 1) as i:
                    for q in range(PAIRS):
                        load(i, q + AHEAD)
                for p in range(PAIRS * (TURNS - 1), NPAIR - AHEAD):
                    load(p // PAIRS, p % PAIRS + AHEAD)
                for h in range(2):
                    sp.wait_ge(wsum_out[h], wsum_stores(h))
                sp.wait_ge(counted, 1)
                for k in range(3):
                    sp.dma_start(wsums[:, k], weight_sums[k, 0:N * NB].rearrange("(b p c) -> p b c", p=P, c=NB)
                                 ).then_inc(wsum_in, 16)
            with sp.Else():
                for k in range(4):
                    if k > 0:
                        if k == 1:
                            sp.wait_ge(dve, at["scaled"])
                        else:
                            sp.wait_ge(state_ready, (k - 1) * NG)
                        sp.dma_start(feat_rows.rearrange("(b p) f -> p b f", p=P), g_rows).then_inc(g_rows_out, 16)
                        sp.wait_ge(g_rows_out, 16 * k)
                    else:
                        sp.wait_ge(dve, at["ones"])
                    with sp.Fori(0, EP) as r:
                        sp.wait_ge(g_added, 4 * (k * EP + r))
                        chunk = lambda a: a[bass.ds(r * P, P)].rearrange("(p o) -> p o", o=1)
                        sp.dma_start(g_idx[:, 0:1], chunk(dst)).then_inc(g_in, 16)
                        sp.dma_start(g_idx[:, 1:2], chunk(src)).then_inc(g_in, 16)
                        sp.dma_start(g_wgt, ew[bass.ds(r * P, P), :]).then_inc(g_in, 16)
            for g in range(NG):
                sp.wait_ge(result_ready, g + 1)
                sp.dma_start(out_v[:, blocks(g), :], xs[:, blocks(g), :]).then_inc(stored, 16)
            sp.wait_ge(stored, 16 * NG)


_INS = ["x", "src", "dst", "edge_weight1", "L0_gnn_W", "L0_gnn_b", "L1_gnn_W_msg", "L1_gnn_b_msg",
        "L1_gnn_W_ih", "L1_gnn_W_hh", "L1_gnn_b_ih", "L1_gnn_b_hh"]


def kernel(**inputs):
    import concourse.bacc as bacc
    from concourse.bass_utils import run_bass_kernel_spmd

    nc = bacc.Bacc("TRN2", target_bir_lowering=False, num_devices=1, dynamic_dma_scratch_size=8192)
    arrays, args = {}, []
    for name in _INS:
        a = np.ascontiguousarray(inputs[name])
        arrays[f"in_{name}"] = a
        args.append(nc.dram_tensor(f"in_{name}", a.shape, mybir.dt.from_np(a.dtype), kind="ExternalInput").ap())
    out = nc.dram_tensor("out", (N, F), F32, kind="ExternalOutput").ap()
    build_program(nc, *args, out)
    return run_bass_kernel_spmd(nc, [arrays], core_ids=[0]).results[0]["out"]
```
